# Optimizing a Trainium2 kernel written in Bass

```python
import numpy as np
import jax
import jax.numpy as jnp

def _softmax(x, axis=-1):
    return jax.nn.softmax(x, axis=axis)

def _gelu(x):
    return jax.nn.gelu(x, approximate=True)

def _silu(x):
    return jax.nn.silu(x)

def _sigmoid(x):
    return jax.nn.sigmoid(x)

def _layernorm(x, axis=-1, eps=1e-05):
    m = jnp.mean(x, axis=axis, keepdims=True)
    v = jnp.var(x, axis=axis, keepdims=True)
    return (x - m) / jnp.sqrt(v + eps)

def _scatter_add(tgt, idx, src, axis=0):
    return tgt.at[idx].add(src)

def _segment_sum(src, seg, n):
    return jax.ops.segment_sum(src, seg, n)
kernel_name = 'mk_adj_preln_d2_adj_r2_b007f1'

def setup_inputs(seed: int=0):
    np.random.seed(seed)
    _w = jnp.asarray

    def _rec_inputs():
        import jax
        import jax.numpy as jnp
        _gk = jax.random.key(seed)
        x = -0.000125 + 0.9999 * jax.random.normal(jax.random.fold_in(_gk, 1), (64, 128, 128), jnp.float32)
        _w = (1.0 + jnp.arange(128, dtype=jnp.float32)) ** (-0.5)
        _w = _w / _w.mean()
        _pij = jnp.clip(0.125 * _w[:, None] * _w[None, :], 0.0, 1.0)
        _a = jax.random.uniform(jax.random.fold_in(_gk, 2), (128, 128)) < _pij
        _a = jnp.logical_or(_a, jnp.swapaxes(_a, -1, -2))
        _a = jnp.logical_or(_a, jnp.eye(128, dtype=bool))
        _af = _a.astype(jnp.float32)
        _af = _af * jax.random.uniform(jax.random.fold_in(_gk, 3), (128, 128), jnp.float32, 0.05, 0.000488281)
        adj = _af
        return (x, adj)
    x, adj = _rec_inputs()

    def _L0_gnn_setup():
        import jax, jax.numpy as jnp
        import numpy as np
        B, T, D, H = (64, 1024, 128, 128)
        MAX_SKIP = 4

        def _lstm_last(Wih, Whh, bih, bhh, xs):
            N, _, Hd = xs.shape
            bias = bih + bhh

            def step(carry, x_t):
                h, c = carry
                g = x_t @ Wih.T + h @ Whh.T + bias
                i, f, gg, o = jnp.split(g, 4, axis=-1)
                c = jax.nn.sigmoid(f) * c + jax.nn.sigmoid(i) * jnp.tanh(gg)
                h = jax.nn.sigmoid(o) * jnp.tanh(c)
                return ((h, c), None)
            init = (jnp.zeros((N, Hd), xs.dtype), jnp.zeros((N, Hd), xs.dtype))
            (h_last, _), _ = jax.lax.scan(step, init, jnp.swapaxes(xs, 0, 1))
            return h_last
        key = jax.random.key(seed)
        ks = jax.random.split(key, 8)
        s = 0.05
        x = jax.random.normal(ks[0], (B, T, D), jnp.float32)
        adj = jax.random.uniform(ks[1], (T, T), jnp.float32) / T
        Wg0 = jax.random.normal(ks[2], (D, H), jnp.float32) * s
        bg0 = jnp.zeros((H,), jnp.float32)
        Wg1 = jax.random.normal(ks[3], (H, H), jnp.float32) * s
        bg1 = jnp.zeros((H,), jnp.float32)
        Wih = jax.random.normal(ks[4], (MAX_SKIP, 4 * H, H), jnp.float32) * s
        Whh = jax.random.normal(ks[5], (MAX_SKIP, 4 * H, H), jnp.float32) * s
        bih = jax.random.normal(ks[6], (MAX_SKIP, 4 * H), jnp.float32) * s
        bhh = jax.random.normal(ks[7], (MAX_SKIP, 4 * H), jnp.float32) * s
        return dict(x=x, adj=adj, Wg0=Wg0, bg0=bg0, Wg1=Wg1, bg1=bg1, Wih=Wih, Whh=Whh, bih=bih, bhh=bhh)
    _L0_gnn_all = _L0_gnn_setup()
    _L0_gnn_in = {k: v for k, v in _L0_gnn_all.items() if k in ('Wg0', 'bg0', 'Wg1', 'bg1', 'Wih', 'Whh', 'bih', 'bhh')}
    del _L0_gnn_all

    def _L1_gnn_setup():
        import jax, jax.numpy as jnp
        import numpy as np
        B, J, F_IN, F_OUT = (8192, 17, 128, 128)
        key = jax.random.key(seed)
        k1, k2, k3, k4 = jax.random.split(key, 4)
        gain = 1.414
        bound = gain * np.sqrt(6.0 / (F_IN + F_OUT))
        W = jax.random.uniform(k2, (3, F_IN, F_OUT), dtype=jnp.float32, minval=-bound, maxval=bound)
        stdv = 1.0 / np.sqrt(F_OUT)
        bias = jax.random.uniform(k4, (F_OUT,), dtype=jnp.float32, minval=-stdv, maxval=stdv)
        return {'x': jax.random.normal(k1, (B, J, F_IN), dtype=jnp.float32), 'W': W, 'adj': jax.random.uniform(k3, (J, J), dtype=jnp.float32), 'bias': bias}
    _L1_gnn_all = _L1_gnn_setup()
    _L1_gnn_in = {k: v for k, v in _L1_gnn_all.items() if k in ('W', 'bias')}
    del _L1_gnn_all
    return {'x': x, 'adj': adj, 'L0_gnn_Wg0': _L0_gnn_in['Wg0'], 'L0_gnn_bg0': _L0_gnn_in['bg0'], 'L0_gnn_Wg1': _L0_gnn_in['Wg1'], 'L0_gnn_bg1': _L0_gnn_in['bg1'], 'L0_gnn_Wih': _L0_gnn_in['Wih'], 'L0_gnn_Whh': _L0_gnn_in['Whh'], 'L0_gnn_bih': _L0_gnn_in['bih'], 'L0_gnn_bhh': _L0_gnn_in['bhh'], 'L1_gnn_W': _L1_gnn_in['W'], 'L1_gnn_bias': _L1_gnn_in['bias']}

def reference(x, adj, L0_gnn_Wg0, L0_gnn_bg0, L0_gnn_Wg1, L0_gnn_bg1, L0_gnn_Wih, L0_gnn_Whh, L0_gnn_bih, L0_gnn_bhh, L1_gnn_W, L1_gnn_bias):
    import jax
    import jax.numpy as jnp

    def _L0_gnn_ref(x, adj, Wg0, bg0, Wg1, bg1, Wih, Whh, bih, bhh):
        import jax, jax.numpy as jnp
        import numpy as np
        B, T, D, H = (64, 1024, 128, 128)
        MAX_SKIP = 4

        def _lstm_last(Wih, Whh, bih, bhh, xs):
            N, _, Hd = xs.shape
            bias = bih + bhh

            def step(carry, x_t):
                h, c = carry
                g = x_t @ Wih.T + h @ Whh.T + bias
                i, f, gg, o = jnp.split(g, 4, axis=-1)
                c = jax.nn.sigmoid(f) * c + jax.nn.sigmoid(i) * jnp.tanh(gg)
                h = jax.nn.sigmoid(o) * jnp.tanh(c)
                return ((h, c), None)
            init = (jnp.zeros((N, Hd), xs.dtype), jnp.zeros((N, Hd), xs.dtype))
            (h_last, _), _ = jax.lax.scan(step, init, jnp.swapaxes(xs, 0, 1))
            return h_last
        h = jax.nn.relu(jnp.einsum('ts,bsh->bth', adj, x @ Wg0 + bg0))
        h = jax.nn.relu(jnp.einsum('ts,bsh->bth', adj, h @ Wg1 + bg1))
        Bv, Tv, Hd = h.shape
        for p in range(1, MAX_SKIP + 1):
            nw = Tv // p
            wins = h[:, :nw * p, :].reshape(Bv * nw, p, Hd)
            last = _lstm_last(Wih[p - 1], Whh[p - 1], bih[p - 1], bhh[p - 1], wins)
            idx = jnp.arange(nw) * p + (p - 1)
            h = h.at[:, idx, :].set(last.reshape(Bv, nw, Hd))
        return h

    def _L1_gnn_ref(x, W, adj, bias):
        import jax, jax.numpy as jnp
        import numpy as np
        B, J, F_IN, F_OUT = (8192, 17, 128, 128)
        adj_0 = jnp.diag(jnp.diagonal(adj))
        adj_1 = jnp.triu(adj, k=1)
        adj_2 = jnp.tril(adj, k=-1)
        h = jnp.einsum('bjf,kfo->kbjo', x, W)
        out = jnp.einsum('ij,bjo->bio', adj_0, h[0]) + jnp.einsum('ij,bjo->bio', adj_1, h[1]) + jnp.einsum('ij,bjo->bio', adj_2, h[2])
        return out + bias[None, None, :]
    h = jnp.maximum(_layernorm(x, axis=-1), 0.0)
    x = x + _L0_gnn_ref(h, adj, L0_gnn_Wg0, L0_gnn_bg0, L0_gnn_Wg1, L0_gnn_bg1, L0_gnn_Wih, L0_gnn_Whh, L0_gnn_bih, L0_gnn_bhh)
    h = jnp.maximum(_layernorm(x, axis=-1), 0.0)
    x = x + _L1_gnn_ref(h, L1_gnn_W, adj, L1_gnn_bias)
    return x

_drawn_inputs = setup_inputs


def setup_inputs(seed=0):
    import zlib

    import numpy as np

    out = dict(_drawn_inputs(seed))
    spreads = {'L0_gnn_bg0': (0.0, 0.8), 'L0_gnn_bg1': (0.0, 0.8)}
    factors = {'L0_gnn_Wg0': 6.16,
     'L0_gnn_Wg1': 3.951,
     'L0_gnn_Wih': 2.943,
     'L0_gnn_Whh': 8.0,
     'L0_gnn_bih': 3.232,
     'L0_gnn_bhh': 3.281}
    for name, (base, spread) in spreads.items():
        noise = np.random.default_rng([zlib.crc32(name.encode()), seed]).standard_normal(out[name].shape)
        drawn = base * np.exp(spread * noise) if base else spread * noise
        out[name] = jnp.asarray(drawn.astype(out[name].dtype))
    for name, factor in factors.items():
        out[name] = (out[name] * factor).astype(out[name].dtype)
    return out
```

```python
from contextlib import ExitStack

import concourse.bass as bass
from concourse import mybir

F32 = mybir.dt.float32
F32R = mybir.dt.float32r
ALU = mybir.AluOpType
ACT = mybir.ActivationFunctionType

B, T, D = 64, 128, 128
G = 16
GROUPS = B // G
HB = G // 2
STREAMS = 2
PACK = 512 // T
HBANKS = HB // PACK
EPS = 1e-5
ADJ_PARTS = 3

I, F, C, O = range(4)
FIRST_STEP = (I, C, O)
LATER_STEP = (I, C, F, O)
SKIPS = (1, 2, 3, 4)


def lstm_units():
    units = []
    for p in SKIPS:
        chunks = max(1, (T // p) * HB // 512)
        nw = (T // p) // chunks
        for c in range(chunks):
            for j in range(p):
                for s in range(STREAMS):
                    units.append((p, s, j, c * nw, nw, FIRST_STEP if j == 0 else LATER_STEP))
    return units


UNITS = lstm_units()
GATES_BEFORE = [sum(len(u[5]) for u in UNITS[:k]) for k in range(len(UNITS) + 1)]
GATES = GATES_BEFORE[-1]
STEPS_OF = [2 if u[5] == FIRST_STEP else 4 for u in UNITS]
STEPS_BEFORE = [sum(STEPS_OF[:k]) for k in range(len(UNITS) + 1)]
STEPS = STEPS_BEFORE[-1]


def last_unit(k, s):
    return next((n for n in range(k - 1, -1, -1) if UNITS[n][1] == s), None)


LAST_OF = [last_unit(len(UNITS), s) for s in range(STREAMS)]

LN_STATS_AT = {k: (2 * k, 2 * k + 1) for k in range(G // 2)}
LN_COMBINE_AT = G // 2
LN_APPLY_AT = {k + 2 + G // 2: (2 * k, 2 * k + 1) for k in range(G // 2)}
LN_RELU_AT = {2 + G // 2 + G // 4: 0, 2 + G: 1}


def program(nc, x_tbd, adj_t, wg0, bg0_col, wg1, bg1, wih_t, whh_t, bih_t, bhh_t, w_l1, bias, out_tbd):
    with ExitStack() as ctx:
        def sb(name, shape, dt=F32):
            return ctx.enter_context(nc.sbuf_tensor(name, shape, dt))

        def sem(name):
            return ctx.enter_context(nc.semaphore(name))

        X = sb("X", [T, B, D])
        H0 = sb("H0", [T, G, D])
        H3 = sb("H3", [T, G, D])
        U = sb("U", [128, STREAMS, HB * T])
        Z = sb("Z", [128, STREAMS, HB * T])
        Y = sb("Y", [T, STREAMS, HB * D])
        UK = sb("UK", [128, 4, ADJ_PARTS * T])
        HH = sb("HH", [128, STREAMS, T, HB], F32R)
        HL = sb("HL", [128, STREAMS, T, HB], F32R)
        SH = sb("SH", [128, STREAMS, 512], F32R)
        SL = sb("SL", [128, STREAMS, 512], F32R)
        GT = sb("GT", [128, STREAMS, 4, 512])
        CS = sb("CS", [128, STREAMS, 512])
        IC = sb("IC", [128, STREAMS, 512])
        TC = sb("TC", [128, STREAMS, 512])
        HT = sb("HT", [128, STREAMS, 512])
        WI = sb("WI", [D, 4, 4 * D])
        WH = sb("WH", [D, 3, 4 * D])
        WIH = sb("WIH", [D, 4, 4 * D], F32R)
        WIL = sb("WIL", [D, 4, 4 * D], F32R)
        WHH = sb("WHH", [D, 3, 4 * D], F32R)
        WHL = sb("WHL", [D, 3, 4 * D], F32R)
        ADJ = sb("ADJ", [T, T])
        ADJ3 = sb("ADJ3", [T, ADJ_PARTS, T])
        WG0 = sb("WG0", [D, D])
        WG1 = sb("WG1", [D, D])
        WL1 = sb("WL1", [D, ADJ_PARTS, D])
        BG0 = sb("BG0", [D, 1])
        BG0T = sb("BG0T", [D, T])
        BG1 = sb("BG1", [T, D])
        BIAS = sb("BIAS", [T, D])
        BI = sb("BI", [D, 16])
        BH = sb("BH", [D, 16])
        BG = sb("BG", [D, 16])
        ONES = sb("ONES", [T, D])
        IDENT = sb("IDENT", [128, 128])
        IDENTR = sb("IDENTR", [128, 128], F32R)
        ST1 = sb("ST1", [T, G, 6])
        MEAN1 = sb("MEAN1", [T, G])
        VE1 = sb("VE1", [T, G])
        RS1 = sb("RS1", [T, G])
        ST2 = sb("ST2", [T, G, 6])
        MEAN2 = sb("MEAN2", [T, G])
        LN = sb("LN", [T, 5, G])
        VE2 = sb("VE2", [T, G])
        RS2 = sb("RS2", [T, G])
        NHALF = sb("NHALF", [T, G])
        PS = ctx.enter_context(nc.psum_tensor("PS", [128, 8, 512], F32))

        x_first = sem("x_first")
        x_rest = sem("x_rest")
        w_adj = sem("w_adj")
        w_gcn = sem("w_gcn")
        w_lstm = sem("w_lstm")
        w_late = sem("w_late")
        consts = sem("consts")
        split_w = sem("split_w")
        bias_ready = sem("bias_ready")
        rowsum_mm = sem("rowsum_mm")
        bn1 = sem("bn1")
        ln_step = sem("ln_step")
        var1 = sem("var1")
        rs1 = sem("rs1")
        norm1 = sem("norm1")
        h0_ready = sem("h0_ready")
        u_mm = sem("u_mm")
        u_sb = sem("u_sb")
        z_mm = sem("z_mm")
        z_sb = sem("z_sb")
        h1_ready = sem("h1_ready")
        y_mm = sem("y_mm")
        evac = sem("evac")
        v_mm = sem("v_mm")
        h_high = sem("h_high")
        h_low = sem("h_low")
        gate_mm = sem("gate_mm")
        gate_act = sem("gate_act")
        lstm_step = sem("lstm_step")
        cell_ready = sem("cell_ready")
        tanh_ready = sem("tanh_ready")
        h_out = sem("h_out")
        t_mm = sem("t_mm")
        x2_ready = sem("x2_ready")
        bn2 = sem("bn2")
        var2 = sem("var2")
        rs2 = sem("rs2")
        norm2 = sem("norm2")
        h3_ready = sem("h3_ready")
        xb_ready = sem("xb_ready")
        uk_mm = sem("uk_mm")
        uk_sb = sem("uk_sb")
        out_mm = sem("out_mm")
        stored = sem("stored")

        Y_EVAC = 2 * HBANKS
        ROUND_EVAC = 4 * HBANKS

        def y_count(g):
            return 0 if isinstance(g, int) and g == 0 else ROUND_EVAC * g - ROUND_EVAC + Y_EVAC

        def out_count(i, more):
            return ROUND_EVAC * i + (2 * Y_EVAC if more else Y_EVAC)

        COMBINE = 5

        def bank(s, n):
            return PS[:, 4 * s + n, :]

        def as_batches(ap):
            return ap.rearrange("p (b t) -> p b t", b=PACK)

        def windows(h, s, p, j, w0, nw):
            first = p * w0 + j
            return h[:, s, first:first + p * (nw - 1) + 1:p, :]

        def wait_apart(eng, sem, count, met, met_count):
            count = count if isinstance(count, int) else eng.snap(count)
            eng.wait_ge(met, met_count)
            eng.wait_ge(sem, count)

        block = ctx.enter_context(nc.Block())

        @block.sync
        def _(sp):
            sp.dma_start(X[:, 0:HB, :], x_tbd[:, 0:HB, :]).then_inc(x_first, 16)
            sp.dma_start(X[:, HB:G, :], x_tbd[:, HB:G, :]).then_inc(x_first, 16)
            sp.dma_start(WG1[:, :], wg1).then_inc(w_gcn, 16)
            sp.dma_start(BG1[:, :], bg1.rearrange("(a n) -> a n", a=1).broadcast_to([T, D])).then_inc(w_gcn, 16)
            sp.dma_start(WI[:, :, :], wih_t).then_inc(w_lstm, 16)
            sp.dma_start(WH[:, :, :], whh_t).then_inc(w_lstm, 16)
            for g in range(1, GROUPS):
                sp.dma_start(X[:, g * G:(g + 1) * G, :], x_tbd[:, g * G:(g + 1) * G, :]).then_inc(x_rest, 16)
            sp.dma_start(WL1[:, :, :], w_l1).then_inc(w_late, 16)
            sp.dma_start(BIAS[:, :], bias.rearrange("(a n) -> a n", a=1).broadcast_to([T, D])).then_inc(w_late, 16)

            def store(i, more):
                for n in range(2 * HBANKS):
                    sp.wait_ge(evac, out_count(i, more) + n + 1)
                    part = bass.ds(i * G + n * PACK, PACK)
                    sp.dma_start(out_tbd[:, part, :], X[:, part, :]).then_inc(stored, 16)

            with sp.Fori(0, GROUPS - 1) as i:
                store(i, True)
            store(GROUPS - 1, False)
            sp.wait_ge(stored, 16 * GROUPS * 2 * HBANKS)

        @block.gpsimd
        def _(pool):
            pool.dma_start(ADJ[:, :], adj_t).then_inc(w_adj, 16)
            pool.dma_start(WG0[:, :], wg0).then_inc(w_adj, 16)
            pool.dma_start(BG0[:, :], bg0_col).then_inc(w_adj, 16)
            pool.dma_start(BI[:, :], bih_t).then_inc(w_adj, 16)
            pool.dma_start(BH[:, :], bhh_t).then_inc(w_adj, 16)
            pool.memset(ONES[:, :], 1.0).then_inc(consts, 1)
            pool.memset(NHALF[:, :], -0.5).then_inc(consts, 1)

            def rstd(ve, var, count, rs, done, lo, hi):
                pool.wait_ge(var, count)
                pool.tensor_tensor(rs[:, lo:hi], ve[:, lo:hi], NHALF[:, lo:hi], ALU.pow).then_inc(done, 1)

            pool.wait_ge(consts, 2)
            rstd(VE1, var1, 2, RS1, rs1, 0, G)

            pool.wait_ge(w_lstm, 32)
            done = 0
            for p in range(4):
                pairs = [(WI[:, p, :], WIH[:, p, :], WIL[:, p, :])]
                if p:
                    pairs.append((WH[:, p - 1, :], WHH[:, p - 1, :], WHL[:, p - 1, :]))
                for w, high, low in pairs:
                    pool.tensor_copy(high, w).then_inc(split_w, 1)
                    done += 1
                    pool.wait_ge(split_w, done)
                    pool.tensor_tensor(low, w, high.bitcast(F32), ALU.subtract).then_inc(split_w, 1)
                    done += 1

            pool.memset(IDENT[:, :], 0.0).then_inc(consts, 1)
            pool.wait_ge(consts, 3)
            pool.affine_select(out=IDENT[:, :], in_=IDENT[:, :], compare_op=ALU.not_equal, fill=1.0,
                               base=0, pattern=[[-1, 128]], channel_multiplier=1).then_inc(consts, 1)
            pool.wait_ge(consts, 4)
            pool.tensor_copy(IDENTR[:, :], IDENT[:, :]).then_inc(consts, 1)
            pool.wait_ge(w_adj, 5 * 16)
            for k, (op, sign) in enumerate(((ALU.is_equal, 1), (ALU.is_gt, 1), (ALU.is_gt, -1))):
                pool.affine_select(out=ADJ3[:, k, :], in_=ADJ[:, :], compare_op=op, fill=0.0,
                                   base=0, pattern=[[-sign, T]], channel_multiplier=sign).then_inc(consts, 1)
            pool.wait_ge(w_late, 32)

            def group(i, more):
                if more:
                    rstd(VE1, var1, 2 * i + 4, RS1, rs1, 0, G)
                for s in range(STREAMS):
                    rstd(VE2, var2, 2 * STREAMS * i + 2 * s + 2, RS2, rs2, HB * s, HB * s + HB)
                    pool.wait_ge(norm2, G * i + HB * (s + 1))
                    part = bass.ds(i * G + s * HB, HB)
                    pool.tensor_tensor(X[:, part, :], X[:, part, :],
                                       BIAS[:, :].unsqueeze(1).broadcast_to([T, HB, D]),
                                       ALU.add).then_inc(xb_ready, 1)

            with pool.Fori(0, GROUPS - 1) as i:
                group(i, True)
            group(GROUPS - 1, False)

        @block.tensor
        def _(pe):
            def graph_u(s, g):
                pe.wait_ge(h0_ready, STREAMS * g + s + 1)
                for n in range(HB):
                    mm = pe.matmul(as_batches(bank(s, 2 + n // PACK))[:, n % PACK, :],
                                   H0[:, s * HB + n, :], ADJ[:, :], start=True, stop=True)
                    if n % PACK == PACK - 1:
                        mm.then_inc(u_mm, 1)

            def graph_z(s, g, after_transpose):
                for n in range(HBANKS):
                    pe.wait_ge(u_sb, 2 * HBANKS * g + s * HBANKS + n + 1)
                    if after_transpose:
                        pe.wait_ge(x2_ready, 2 * HBANKS * (g - 1) + s * HBANKS + n + 1)
                    pe.matmul(bank(s, n), WG0[:, :], U[:, s, 512 * n:512 * n + 512],
                              start=True, stop=True).then_inc(z_mm, 1)

            def graph_y(s, g):
                for n in range(HB):
                    if n % PACK == 0:
                        pe.wait_ge(h1_ready, 2 * HBANKS * g + s * HBANKS + n // PACK + 1)
                    mm = pe.matmul(as_batches(bank(s, 2 + n // PACK))[:, n % PACK, :],
                                   Z[:, s, T * n:T * n + T], WG1[:, :], start=True, stop=True)
                    if n % PACK == PACK - 1:
                        mm.then_inc(y_mm, 1)

            def graph_v(s, g):
                for n in range(HB):
                    if n % PACK == 0:
                        pe.wait_ge(evac, y_count(g) + s * HBANKS + n // PACK + 1)
                    mm = pe.matmul(as_batches(bank(s, n // PACK))[:, n % PACK, :],
                                   Y[:, s, D * n:D * n + D], ADJ[:, :], start=True, stop=True)
                    if n % PACK == PACK - 1:
                        mm.then_inc(v_mm, 1)

            def unit(k, i):
                p, s, j, w0, nw, gates = UNITS[k]
                prev = last_unit(k, s)
                n = nw * HB
                if prev is None:
                    pe.wait_ge(h_high, 2 * HBANKS * i + HBANKS * (s + 1))
                    pe.wait_ge(h_low, 2 * HBANKS * i + HBANKS * (s + 1))
                    pe.wait_ge(evac, Y_EVAC + ROUND_EVAC * i)
                elif j == 0 and p > 1:
                    pe.wait_ge(h_out, len(UNITS) * i + prev + 1)
                x_high, x_low = windows(HH, s, p, j, w0, nw), windows(HL, s, p, j, w0, nw)
                for q in gates:
                    if prev is not None:
                        read = UNITS[prev][5].index(q) if q in UNITS[prev][5] else 0
                        pe.wait_ge(gate_act, GATES * i + GATES_BEFORE[prev] + read + 1)
                    dst = bank(s, q)[:, 0:n].rearrange("p (w b) -> p w b", b=HB)
                    cols = slice(q * D, q * D + D)
                    pe.matmul(dst, WIH[:, p - 1, cols], x_high, start=True, stop=False)
                    pe.matmul(dst, WIL[:, p - 1, cols], x_high, start=False, stop=False)
                    mm = pe.matmul(dst, WIH[:, p - 1, cols], x_low, start=False, stop=(j == 0))
                    if j == 0:
                        mm.then_inc(gate_mm, 1)
                if j > 0:
                    pe.wait_ge(h_out, len(UNITS) * i + prev + 1)
                    for q in gates:
                        dst = bank(s, q)[:, 0:n]
                        cols = slice(q * D, q * D + D)
                        pe.matmul(dst, WHH[:, p - 2, cols], SH[:, s, 0:n], start=False, stop=False)
                        pe.matmul(dst, WHL[:, p - 2, cols], SH[:, s, 0:n], start=False, stop=False)
                        pe.matmul(dst, WHH[:, p - 2, cols], SL[:, s, 0:n], start=False,
                                  stop=True).then_inc(gate_mm, 1)

            def transpose_h(s, i):
                pe.wait_ge(h_out, len(UNITS) * i + LAST_OF[s] + 1)
                for n in range(HB):
                    dst = as_batches(bank(s, n // PACK))[:, n % PACK, :]
                    pe.matmul(dst, HH[:, s, :, n], IDENTR[:, :], start=True, stop=False)
                    mm = pe.matmul(dst, HL[:, s, :, n], IDENTR[:, :], start=False, stop=True)
                    if n % PACK == PACK - 1:
                        mm.then_inc(t_mm, 1)

            def last_layer(i, more):
                lag = 2
                ring = [(0, 2), (0, 3), (1, 2), (1, 3)]
                for n in range(G + lag):
                    if n < G:
                        if n % HB == 0:
                            pe.wait_ge(h3_ready, STREAMS * i + n // HB + 1)
                        s, c = ring[n % 4]
                        pe.matmul(bank(s, c)[:, 0:ADJ_PARTS * T], H3[:, n, :],
                                  ADJ3[:, :, :].rearrange("p k t -> p (k t)"),
                                  start=True, stop=True).then_inc(uk_mm, 1)
                    m = n - lag
                    if m >= 0:
                        s, c = m // HB, m % HB // PACK
                        if m % PACK == 0 and more:
                            pe.wait_ge(h_low, 2 * HBANKS * (i + 1) + m // PACK + 1)
                        pe.wait_ge(uk_sb, G * i + m + 1)
                        for k in range(ADJ_PARTS):
                            mm = pe.matmul(as_batches(bank(s, c))[:, m % PACK, :],
                                           UK[:, m % 4, k * T:(k + 1) * T], WL1[:, k, :],
                                           start=(k == 0), stop=(k == ADJ_PARTS - 1))
                        if m % PACK == PACK - 1:
                            mm.then_inc(out_mm, 1)

            pe.wait_ge(w_adj, 5 * 16)
            pe.wait_ge(w_gcn, 2 * 16)
            pe.wait_ge(consts, 2)
            pe.matmul(bank(0, 0)[:, 0:T], ONES[:, :], ADJ[:, :], start=True, stop=True).then_inc(rowsum_mm, 1)
            for s in range(STREAMS):
                graph_u(s, 0)
            pe.wait_ge(bias_ready, 2)
            for s in range(STREAMS):
                graph_z(s, 0, False)
            for s in range(STREAMS):
                graph_y(s, 0)
            for s in range(STREAMS):
                graph_v(s, 0)
            pe.wait_ge(split_w, 14)
            pe.wait_ge(consts, 8)
            pe.wait_ge(w_late, 32)

            def group(i, more):
                for k in range(len(UNITS)):
                    unit(k, i)
                transpose_h(0, i)
                if more:
                    graph_u(0, i + 1)
                    pe.wait_ge(gate_act, GATES * i + GATES)
                    graph_u(1, i + 1)
                transpose_h(1, i)
                if more:
                    graph_z(0, i + 1, True)
                    graph_z(1, i + 1, True)
                    for s in range(STREAMS):
                        graph_y(s, i + 1)
                    for s in range(STREAMS):
                        graph_v(s, i + 1)
                last_layer(i, more)

            with pe.Fori(0, GROUPS - 1) as i:
                group(i, True)
            group(GROUPS - 1, False)

        @block.scalar
        def _(act):
            def relu_h0(s, g):
                act.wait_ge(norm1, G * g + HB * (s + 1))
                part = H0[:, s * HB:(s + 1) * HB, :]
                act.activation(part, part, ACT.Relu).then_inc(h0_ready, 1)

            def copy_u(s, g):
                for n in range(HBANKS):
                    act.wait_ge(u_mm, 2 * HBANKS * g + s * HBANKS + n + 1)
                    act.activation(U[:, s, 512 * n:512 * n + 512], bank(s, 2 + n), ACT.Copy).then_inc(u_sb, 1)

            def relu_z(s, g):
                for n in range(HBANKS):
                    act.wait_ge(z_sb, 2 * HBANKS * g + s * HBANKS + n + 1)
                    part = Z[:, s, 512 * n:512 * n + 512]
                    act.activation(part, part, ACT.Relu).then_inc(h1_ready, 1)

            def high_h(s, g):
                for n in range(HBANKS):
                    act.wait_ge(v_mm, 2 * HBANKS * g + s * HBANKS + n + 1)
                    act.activation(HH[:, s, :, n * PACK:(n + 1) * PACK].rearrange("p t b -> p b t"),
                                   as_batches(bank(s, n)), ACT.Relu).then_inc(h_high, 1)

            def unit(k, i):
                p, s, j, w0, nw, gates = UNITS[k]
                prev = last_unit(k, s)
                n = nw * HB
                if p == 1 and prev is not None:
                    act.wait_ge(h_out, len(UNITS) * i + prev + 1)
                for m, q in enumerate(gates):
                    act.wait_ge(gate_mm, GATES * i + GATES_BEFORE[k] + m + 1)
                    act.activation(GT[:, s, q, 0:n], bank(s, q)[:, 0:n],
                                   ACT.Tanh if q == C else ACT.Sigmoid,
                                   bias=BG[:, 4 * (p - 1) + q:4 * (p - 1) + q + 1]).then_inc(gate_act, 1)
                act.wait_ge(cell_ready, len(UNITS) * i + k + 1)
                act.activation(TC[:, s, 0:n], CS[:, s, 0:n], ACT.Tanh).then_inc(tanh_ready, 1)

            def relu_h3(s, i):
                act.wait_ge(norm2, G * i + HB * (s + 1))
                part = H3[:, s * HB:(s + 1) * HB, :]
                act.activation(part, part, ACT.Relu).then_inc(h3_ready, 1)

            def copy_uk(i):
                ring = [(0, 2), (0, 3), (1, 2), (1, 3)]
                for n in range(G):
                    act.wait_ge(uk_mm, G * i + n + 1)
                    s, c = ring[n % 4]
                    act.activation(UK[:, n % 4, :], bank(s, c)[:, 0:ADJ_PARTS * T], ACT.Copy).then_inc(uk_sb, 1)

            relu_h0(0, 0)
            relu_h0(1, 0)
            for part in (copy_u, relu_z, high_h):
                part(0, 0)
                part(1, 0)
            act.wait_ge(bias_ready, 1)

            def group(i, more):
                for k in range(len(UNITS)):
                    unit(k, i)
                    if more and k in LN_RELU_AT:
                        relu_h0(LN_RELU_AT[k], i + 1)
                if more:
                    copy_u(0, i + 1)
                    copy_u(1, i + 1)
                    relu_z(0, i + 1)
                    relu_z(1, i + 1)
                    high_h(0, i + 1)
                    relu_h3(0, i)
                    high_h(1, i + 1)
                    relu_h3(1, i)
                else:
                    relu_h3(0, i)
                    relu_h3(1, i)
                copy_uk(i)

            with act.Fori(0, GROUPS - 1) as i:
                group(i, True)
            group(GROUPS - 1, False)

        @block.vector
        def _(dve):
            def stats1(g, batches):
                for b in batches:
                    dve.bn_stats(ST1[:, b, :], X[:, g * G + b, :]).then_inc(bn1, 1)

            def combine(st, done, count, before, mean, ve, var, lo, hi):
                diff, total, spread, square, both = (LN[:, n, lo:hi] for n in range(5))
                dve.wait_ge(done, count)
                dve.tensor_tensor(diff, st[:, lo:hi, 1], st[:, lo:hi, 4], ALU.subtract).then_inc(ln_step, 1)
                dve.tensor_tensor(total, st[:, lo:hi, 1], st[:, lo:hi, 4], ALU.add).then_inc(ln_step, 1)
                dve.tensor_tensor(spread, st[:, lo:hi, 2], st[:, lo:hi, 5], ALU.add).then_inc(ln_step, 1)
                dve.wait_ge(ln_step, before + 1)
                dve.tensor_tensor(square, diff, diff, ALU.mult).then_inc(ln_step, 1)
                dve.wait_ge(ln_step, before + 2)
                dve.tensor_scalar(mean[:, lo:hi], total, 0.5, None, ALU.mult).then_inc(var, 1)
                dve.wait_ge(ln_step, before + 4)
                dve.scalar_tensor_tensor(out=both, in0=square, scalar=D / 4, in1=spread,
                                         op0=ALU.mult, op1=ALU.add).then_inc(ln_step, 1)
                dve.wait_ge(ln_step, before + 5)
                dve.tensor_scalar(ve[:, lo:hi], both, 1 / D, EPS, ALU.mult, ALU.add).then_inc(var, 1)

            def norm_h0(g, batches):
                dve.wait_ge(rs1, g + 1)
                for b in batches:
                    dve.tensor_scalar(H0[:, b, :], X[:, g * G + b, :], MEAN1[:, b:b + 1], RS1[:, b:b + 1],
                                      ALU.subtract, ALU.mult).then_inc(norm1, 1)

            def bias_z(s, g):
                for n in range(HBANKS):
                    dve.wait_ge(z_mm, 2 * HBANKS * g + s * HBANKS + n + 1)
                    dve.tensor_tensor(as_batches(Z[:, s, 512 * n:512 * n + 512]), as_batches(bank(s, n)),
                                      BG0T[:, :].unsqueeze(1).broadcast_to([128, PACK, T]),
                                      ALU.add).then_inc(z_sb, 1)

            def bias_y(s, g):
                for n in range(HBANKS):
                    dve.wait_ge(y_mm, 2 * HBANKS * g + s * HBANKS + n + 1)
                    dve.tensor_tensor(as_batches(Y[:, s, 512 * n:512 * n + 512]), as_batches(bank(s, 2 + n)),
                                      BG1[:, :].unsqueeze(1).broadcast_to([128, PACK, D]),
                                      ALU.add).then_inc(evac, 1)

            def low_h(s, g):
                for n in range(HBANKS):
                    dve.wait_ge(h_high, 2 * HBANKS * g + s * HBANKS + n + 1)
                    part = slice(n * PACK, (n + 1) * PACK)
                    dve.scalar_tensor_tensor(out=HL[:, s, :, part].rearrange("p t b -> p b t"),
                                             in0=as_batches(bank(s, n)), scalar=0.0,
                                             in1=HH[:, s, :, part].rearrange("p t b -> p b t").bitcast(F32),
                                             op0=ALU.max, op1=ALU.subtract).then_inc(h_low, 1)

            def unit_cell(k, i):
                p, s, j, w0, nw, gates = UNITS[k]
                n = nw * HB
                done = GATES * i + GATES_BEFORE[k]
                steps = STEPS * i + STEPS_BEFORE[k]
                dve.wait_ge(gate_act, done + 2)
                if j == 0:
                    dve.tensor_tensor(CS[:, s, 0:n], GT[:, s, I, 0:n], GT[:, s, C, 0:n],
                                      ALU.mult).then_inc(cell_ready, 1)
                    return
                dve.tensor_tensor(IC[:, s, 0:n], GT[:, s, I, 0:n], GT[:, s, C, 0:n],
                                  ALU.mult).then_inc(lstm_step, 1)
                dve.wait_ge(gate_act, done + 3)
                dve.tensor_tensor(CS[:, s, 0:n], GT[:, s, F, 0:n], CS[:, s, 0:n],
                                  ALU.mult).then_inc(lstm_step, 1)
                dve.wait_ge(lstm_step, steps + 2)
                dve.tensor_tensor(CS[:, s, 0:n], IC[:, s, 0:n], CS[:, s, 0:n],
                                  ALU.add).then_inc(cell_ready, 1)

            def unit_hidden(k, i):
                p, s, j, w0, nw, gates = UNITS[k]
                n = nw * HB
                steps = STEPS * i + STEPS_BEFORE[k] + STEPS_OF[k]
                dve.wait_ge(tanh_ready, len(UNITS) * i + k + 1)
                dve.tensor_tensor(HT[:, s, 0:n], GT[:, s, O, 0:n], TC[:, s, 0:n],
                                  ALU.mult).then_inc(lstm_step, 1)
                if j == p - 1:
                    high, low = windows(HH, s, p, j, w0, nw), windows(HL, s, p, j, w0, nw)
                    full = HT[:, s, 0:n].rearrange("p (w b) -> p w b", b=HB)
                else:
                    high, low, full = SH[:, s, 0:n], SL[:, s, 0:n], HT[:, s, 0:n]
                dve.wait_ge(lstm_step, steps - 1)
                dve.tensor_copy(high, full).then_inc(lstm_step, 1)
                dve.wait_ge(lstm_step, steps)
                dve.tensor_tensor(low, full, high.bitcast(F32), ALU.subtract).then_inc(h_out, 1)

            def add_x(s, i):
                for n in range(HBANKS):
                    dve.wait_ge(t_mm, 2 * HBANKS * i + s * HBANKS + n + 1)
                    part = bass.ds(i * G + s * HB + n * PACK, PACK)
                    dve.tensor_tensor(X[:, part, :], as_batches(bank(s, n)), X[:, part, :],
                                      ALU.add).then_inc(x2_ready, 1)

            def stats2(s, i, more):
                wait_apart(dve, x2_ready, 2 * HBANKS * i + HBANKS * (s + 1), x_first, 32)
                for b in range(s * HB, s * HB + HB):
                    dve.bn_stats(ST2[:, b, :], X[:, i * G + b, :]).then_inc(bn2, 1)
                combine(ST2, bn2, G * i + HB * (s + 1), COMBINE * (3 * i + s + (2 if more else 1)),
                        MEAN2, VE2, var2, s * HB, s * HB + HB)

            def norm_h3(s, i):
                dve.wait_ge(rs2, STREAMS * i + s + 1)
                for b in range(s * HB, s * HB + HB):
                    dve.tensor_scalar(H3[:, b, :], X[:, i * G + b, :], MEAN2[:, b:b + 1], RS2[:, b:b + 1],
                                      ALU.subtract, ALU.mult).then_inc(norm2, 1)

            def add_out(i, n):
                dve.wait_ge(out_mm, 2 * HBANKS * i + n + 1)
                dve.wait_ge(xb_ready, STREAMS * i + n // HBANKS + 1)
                part = bass.ds(i * G + n * PACK, PACK)
                dve.tensor_tensor(X[:, part, :], as_batches(bank(n // HBANKS, n % HBANKS)), X[:, part, :],
                                  ALU.add).then_inc(evac, 1)

            dve.wait_ge(x_first, 32)
            stats1(0, range(G))
            combine(ST1, bn1, G, 0, MEAN1, VE1, var1, 0, G)
            norm_h0(0, range(G))
            dve.wait_ge(w_adj, 5 * 16)
            dve.wait_ge(w_gcn, 2 * 16)
            dve.tensor_tensor(BG[:, :], BI[:, :], BH[:, :], ALU.add).then_inc(bias_ready, 1)
            dve.wait_ge(rowsum_mm, 1)
            dve.tensor_scalar(BG0T[:, :], bank(0, 0)[:, 0:T], BG0[:, 0:1], None, ALU.mult).then_inc(bias_ready, 1)
            dve.wait_ge(bias_ready, 2)
            for part in (bias_z, bias_y, low_h):
                part(0, 0)
                part(1, 0)
            dve.wait_ge(x_rest, 16 * (GROUPS - 1))

            def group(i, more):
                for k in range(len(UNITS)):
                    unit_cell(k, i)
                    if more and k in LN_STATS_AT:
                        stats1(i + 1, LN_STATS_AT[k])
                    if more and k == LN_COMBINE_AT:
                        combine(ST1, bn1, G * i + 2 * G, COMBINE * (3 * i + 1), MEAN1, VE1, var1, 0, G)
                    if more and k in LN_APPLY_AT:
                        norm_h0(i + 1, LN_APPLY_AT[k])
                    unit_hidden(k, i)
                add_x(0, i)
                stats2(0, i, more)
                add_x(1, i)
                if more:
                    bias_z(0, i + 1)
                    bias_z(1, i + 1)
                    stats2(1, i, more)
                    bias_y(0, i + 1)
                    norm_h3(0, i)
                    bias_y(1, i + 1)
                    low_h(0, i + 1)
                    low_h(1, i + 1)
                    norm_h3(1, i)
                else:
                    norm_h3(0, i)
                    stats2(1, i, more)
                    norm_h3(1, i)
                for n in range(2 * HBANKS):
                    add_out(i, n)

            with dve.Fori(0, GROUPS - 1) as i:
                group(i, True)
            group(GROUPS - 1, False)


def kernel(**inputs):
    import numpy as np
    import concourse.bacc as bacc
    from concourse import mybir as _mybir
    from concourse.bass_utils import run_bass_kernel_spmd

    a = {k: np.asarray(v) for k, v in inputs.items()}

    def gates_t(w):
        return w.transpose(2, 0, 1)

    laid_out = {
        "x_tbd": a["x"].transpose(1, 0, 2),
        "adj_t": a["adj"].T,
        "wg0": a["L0_gnn_Wg0"],
        "bg0_col": a["L0_gnn_bg0"].reshape(D, 1),
        "wg1": a["L0_gnn_Wg1"],
        "bg1": a["L0_gnn_bg1"],
        "wih_t": gates_t(a["L0_gnn_Wih"]),
        "whh_t": gates_t(a["L0_gnn_Whh"][1:]),
        "bih_t": a["L0_gnn_bih"].reshape(16, D).T,
        "bhh_t": a["L0_gnn_bhh"].reshape(16, D).T,
        "w_l1": a["L1_gnn_W"].transpose(1, 0, 2),
        "bias": a["L1_gnn_bias"],
    }
    nc = bacc.Bacc("TRN2", target_bir_lowering=False, num_devices=1)
    arrays, args = {}, []
    for name, v in laid_out.items():
        v = np.ascontiguousarray(v)
        arrays[name] = v
        args.append(nc.dram_tensor(name, v.shape, _mybir.dt.from_np(v.dtype), kind="ExternalInput").ap())
    args.append(nc.dram_tensor("out_tbd", (T, B, D), _mybir.dt.float32, kind="ExternalOutput").ap())
    program(nc, *args)
    r = run_bass_kernel_spmd(nc, [arrays], core_ids=[0])
    return np.ascontiguousarray(r.results[0]["out_tbd"].transpose(1, 0, 2))
```

```python
from contextlib import ExitStack

import concourse.bass as bass
from concourse import mybir

F32 = mybir.dt.float32
F32R = mybir.dt.float32r
ALU = mybir.AluOpType
ACT = mybir.ActivationFunctionType

B, T, D = 64, 128, 128
G = 16
GROUPS = B // G
HB = G // 2
STREAMS = 2
PACK = 512 // T
HBANKS = HB // PACK
EPS = 1e-5
ADJ_PARTS = 3

I, F, C, O = range(4)
FIRST_STEP = (I, C, O)
LATER_STEP = (I, C, F, O)
SKIPS = (1, 2, 3, 4)


def lstm_units():
    units = []
    for p in SKIPS:
        chunks = max(1, (T // p) * HB // 512)
        nw = (T // p) // chunks
        for c in range(chunks):
            for j in range(p):
                for s in range(STREAMS):
                    units.append((p, s, j, c * nw, nw, FIRST_STEP if j == 0 else LATER_STEP))
    return units


UNITS = lstm_units()
GATES_BEFORE = [sum(len(u[5]) for u in UNITS[:k]) for k in range(len(UNITS) + 1)]
GATES = GATES_BEFORE[-1]
STEPS_OF = [2 if u[5] == FIRST_STEP else 4 for u in UNITS]
STEPS_BEFORE = [sum(STEPS_OF[:k]) for k in range(len(UNITS) + 1)]
STEPS = STEPS_BEFORE[-1]


def last_unit(k, s):
    return next((n for n in range(k - 1, -1, -1) if UNITS[n][1] == s), None)


LAST_OF = [last_unit(len(UNITS), s) for s in range(STREAMS)]

ADJP, OUTP = "adj", "out"


def both(n):
    return (ADJP, n), (OUTP, n - 1)


LAST_AT = {(1, 1): ((ADJP, 0),), (2, 0): both(1), (2, 1): both(2), (2, 2): both(3),
           (3, 0): both(4), (3, 1): both(5), (3, 2): both(6), (4, 0): both(7),
           (4, 1): both(8), (4, 2): both(9), (5, 0): both(10), (5, 1): ((OUTP, 10),),
           (7, 4): ((ADJP, 11),), (9, 0): both(12), (10, 0): ((OUTP, 12),),
           (13, 4): ((ADJP, 13),), (15, 0): both(14), (16, 0): both(15), (16, 1): ((OUTP, 15),)}
AFTER_F = (11, 13)
CHUNKS = ((0, 3), (3, 3), (6, 3), (9, 2), (11, 2), (13, 3))
CHUNK_AFTER = {2: 0, 3: 1, 4: 2, 5: 3}
CHUNK_AHEAD = {10: 4, 16: 5}
OUT_BEFORE = {7: 4, 11: 5, 17: 6}


def chunk_of(n):
    c = next(c for c, (first, size) in enumerate(CHUNKS) if first <= n < first + size)
    return c, n == CHUNKS[c][0], n == sum(CHUNKS[c]) - 1


LN_STATS_AT = {4 + k: (2 * k, 2 * k + 1) for k in range(G // 2)}
LN_COMBINE_AT = 4 + G // 2
LN_APPLY_AT = {14 + k: range(3 * k, min(3 * k + 3, G)) for k in range(6)}
LN_RELU_AT = {16: 0, 19: 1}


def program(nc, x_tbd, adj_t, wg0, bg0_col, wg1, bg1, wih_t, whh_t, bih_t, bhh_t, w_l1, bias, out_tbd):
    with ExitStack() as ctx:
        def sb(name, shape, dt=F32):
            return ctx.enter_context(nc.sbuf_tensor(name, shape, dt))

        def sem(name):
            return ctx.enter_context(nc.semaphore(name))

        X = sb("X", [T, B, D])
        H0 = sb("H0", [T, G, D])
        H3 = sb("H3", [T, G, D])
        U = sb("U", [128, STREAMS, HB * T])
        Z = sb("Z", [128, STREAMS, HB * T])
        Y = sb("Y", [T, STREAMS, HB * D])
        UK = sb("UK", [128, 4, ADJ_PARTS * T])
        HH = sb("HH", [128, STREAMS, T, HB], F32R)
        HL = sb("HL", [128, STREAMS, T, HB], F32R)
        SH = sb("SH", [128, STREAMS, 512], F32R)
        SL = sb("SL", [128, STREAMS, 512], F32R)
        GT = sb("GT", [128, STREAMS, 4, 512])
        CS = sb("CS", [128, STREAMS, 512])
        IC = sb("IC", [128, STREAMS, 512])
        TC = sb("TC", [128, STREAMS, 512])
        HT = sb("HT", [128, STREAMS, 512])
        WI = sb("WI", [D, 4, 4 * D])
        WH = sb("WH", [D, 3, 4 * D])
        WIH = sb("WIH", [D, 4, 4 * D], F32R)
        WIL = sb("WIL", [D, 4, 4 * D], F32R)
        WHH = sb("WHH", [D, 3, 4 * D], F32R)
        WHL = sb("WHL", [D, 3, 4 * D], F32R)
        ADJ = sb("ADJ", [T, T])
        ADJ3 = sb("ADJ3", [T, ADJ_PARTS, T])
        WG0 = sb("WG0", [D, D])
        WG1 = sb("WG1", [D, D])
        WL1 = sb("WL1", [D, ADJ_PARTS, D])
        BG0 = sb("BG0", [D, 1])
        BG0T = sb("BG0T", [D, T])
        BG1 = sb("BG1", [T, D])
        BIAS = sb("BIAS", [T, D])
        BI = sb("BI", [D, 16])
        BH = sb("BH", [D, 16])
        BG = sb("BG", [D, 16])
        ONES = sb("ONES", [T, D])
        IDENT = sb("IDENT", [128, 128])
        IDENTR = sb("IDENTR", [128, 128], F32R)
        ST1 = sb("ST1", [T, G, 6])
        MINUS1 = sb("MINUS1", [T, G])
        SHIFT1 = sb("SHIFT1", [T, HB])
        VE1 = sb("VE1", [T, G])
        RS1 = sb("RS1", [T, G])
        ST2 = sb("ST2", [T, G, 6])
        MINUS2 = sb("MINUS2", [T, G])
        SHIFT2 = sb("SHIFT2", [T, HB])
        LN = sb("LN", [T, 5, G])
        VE2 = sb("VE2", [T, G])
        RS2 = sb("RS2", [T, G])
        NHALF = sb("NHALF", [T, G])
        PS = ctx.enter_context(nc.psum_tensor("PS", [128, 8, 512], F32))

        x_first = sem("x_first")
        x_second = sem("x_second")
        x_rest = sem("x_rest")
        w_adj = sem("w_adj")
        w_gcn = sem("w_gcn")
        w_lstm = sem("w_lstm")
        w_late = sem("w_late")
        consts = sem("consts")
        split_w = sem("split_w")
        bias_ready = sem("bias_ready")
        rowsum_mm = sem("rowsum_mm")
        bn1 = sem("bn1")
        ln_step = sem("ln_step")
        var1 = sem("var1")
        rs1 = sem("rs1")
        shift1 = sem("shift1")
        norm1 = sem("norm1")
        h0_first = sem("h0_first")
        h0_ready = sem("h0_ready")
        u_mm = sem("u_mm")
        u_sb = sem("u_sb")
        z_mm = sem("z_mm")
        z_sb = sem("z_sb")
        h1_ready = sem("h1_ready")
        y_mm = sem("y_mm")
        y_sb = sem("y_sb")
        out_ready = sem("out_ready")
        v_mm = sem("v_mm")
        h_high = sem("h_high")
        h_low = sem("h_low")
        gate_mm = sem("gate_mm")
        gate_act = sem("gate_act")
        lstm_step = sem("lstm_step")
        cell_ready = sem("cell_ready")
        tanh_ready = sem("tanh_ready")
        h_out = sem("h_out")
        t_mm = sem("t_mm")
        x2_ready = sem("x2_ready")
        bn2 = sem("bn2")
        var2 = sem("var2")
        rs2 = sem("rs2")
        shift2 = sem("shift2")
        norm2 = sem("norm2")
        h3_first = sem("h3_first")
        h3_second = sem("h3_second")
        xb_ready = sem("xb_ready")
        uk_mm = sem("uk_mm")
        uk_sb = sem("uk_sb")
        out_mm = sem("out_mm")
        stored = sem("stored")

        COMBINE = 5

        def bank(s, n):
            return PS[:, 4 * s + n, :]

        def as_batches(ap):
            return ap.rearrange("p (b t) -> p b t", b=PACK)

        def windows(h, s, p, j, w0, nw):
            first = p * w0 + j
            return h[:, s, first:first + p * (nw - 1) + 1:p, :]

        def wait_apart(eng, sem, count, met, met_count):
            count = count if isinstance(count, int) else eng.snap(count)
            eng.wait_ge(met, met_count)
            eng.wait_ge(sem, count)

        block = ctx.enter_context(nc.Block())

        @block.sync
        def _(sp):
            sp.dma_start(X[:, 0:HB, :], x_tbd[:, 0:HB, :]).then_inc(x_first, 16)
            sp.dma_start(X[:, HB:G, :], x_tbd[:, HB:G, :]).then_inc(x_second, 16)
            sp.dma_start(ADJ[:, :], adj_t).then_inc(w_adj, 16)
            sp.dma_start(WG0[:, :], wg0).then_inc(w_adj, 16)
            sp.dma_start(BG0[:, :], bg0_col).then_inc(w_adj, 16)
            sp.dma_start(WG1[:, :], wg1).then_inc(w_gcn, 16)
            sp.dma_start(BG1[:, :], bg1.rearrange("(a n) -> a n", a=1).broadcast_to([T, D])).then_inc(w_gcn, 16)
            sp.dma_start(BI[:, :], bih_t).then_inc(w_gcn, 16)
            sp.dma_start(BH[:, :], bhh_t).then_inc(w_gcn, 16)
            sp.dma_start(WI[:, :, :], wih_t).then_inc(w_lstm, 16)
            sp.dma_start(WH[:, :, :], whh_t).then_inc(w_lstm, 16)
            sp.dma_start(WL1[:, :, :], w_l1).then_inc(w_late, 16)
            sp.dma_start(BIAS[:, :], bias.rearrange("(a n) -> a n", a=1).broadcast_to([T, D])).then_inc(w_late, 16)
            for g in range(1, GROUPS):
                sp.dma_start(X[:, g * G:(g + 1) * G, :], x_tbd[:, g * G:(g + 1) * G, :]).then_inc(x_rest, 16)

            with sp.Fori(0, GROUPS) as i:
                for c, (first, size) in enumerate(CHUNKS):
                    sp.wait_ge(out_ready, len(CHUNKS) * i + c + 1)
                    part = bass.ds(i * G + first, size)
                    sp.dma_start(out_tbd[:, part, :], X[:, part, :]).then_inc(stored, 16)
            sp.wait_ge(stored, 16 * GROUPS * len(CHUNKS))

        @block.gpsimd
        def _(pool):
            pool.memset(ONES[:, :], 1.0).then_inc(consts, 1)
            pool.memset(NHALF[:, :], -0.5).then_inc(consts, 1)

            def rstd(ve, var, count, rs, done, lo, hi):
                pool.wait_ge(var, count)
                pool.tensor_tensor(rs[:, lo:hi], ve[:, lo:hi], NHALF[:, lo:hi], ALU.pow).then_inc(done, 1)

            pool.wait_ge(consts, 2)
            for s in range(STREAMS):
                rstd(VE1, var1, 2 * s + 2, RS1, rs1, HB * s, HB * s + HB)
                if s == 0:
                    pool.wait_ge(rs1, 1)
                    pool.tensor_tensor(SHIFT1[:, :], MINUS1[:, 0:HB], RS1[:, 0:HB], ALU.mult).then_inc(shift1, 1)

            pool.wait_ge(w_lstm, 32)
            done = 0
            for p in range(4):
                pairs = [(WI[:, p, :], WIH[:, p, :], WIL[:, p, :])]
                if p:
                    pairs.append((WH[:, p - 1, :], WHH[:, p - 1, :], WHL[:, p - 1, :]))
                for w, high, low in pairs:
                    pool.tensor_copy(high, w).then_inc(split_w, 1)
                    done += 1
                    pool.wait_ge(split_w, done)
                    pool.tensor_tensor(low, w, high.bitcast(F32), ALU.subtract).then_inc(split_w, 1)
                    done += 1

            pool.memset(IDENT[:, :], 0.0).then_inc(consts, 1)
            pool.wait_ge(consts, 3)
            pool.affine_select(out=IDENT[:, :], in_=IDENT[:, :], compare_op=ALU.not_equal, fill=1.0,
                               base=0, pattern=[[-1, 128]], channel_multiplier=1).then_inc(consts, 1)
            pool.wait_ge(consts, 4)
            pool.tensor_copy(IDENTR[:, :], IDENT[:, :]).then_inc(consts, 1)
            pool.wait_ge(w_adj, 3 * 16)
            for k, (op, sign) in enumerate(((ALU.is_equal, 1), (ALU.is_gt, 1), (ALU.is_gt, -1))):
                pool.affine_select(out=ADJ3[:, k, :], in_=ADJ[:, :], compare_op=op, fill=0.0,
                                   base=0, pattern=[[-sign, T]], channel_multiplier=sign).then_inc(consts, 1)
            pool.wait_ge(w_late, 32)

            def group(i, more):
                if more:
                    rstd(VE1, var1, 2 * i + 6, RS1, rs1, 0, G)
                for s in range(STREAMS):
                    rstd(VE2, var2, 2 * STREAMS * i + 2 * s + 2, RS2, rs2, HB * s, HB * s + HB)
                    if s == 0:
                        pool.wait_ge(rs2, STREAMS * i + 1)
                        pool.tensor_tensor(SHIFT2[:, :], MINUS2[:, 0:HB], RS2[:, 0:HB], ALU.mult).then_inc(shift2, 1)
                for s in range(STREAMS):
                    if s == 0:
                        pool.wait_ge(h3_first, HB * i + HB)
                    else:
                        pool.wait_ge(norm2, HB * i + HB)
                    part = bass.ds(i * G + s * HB, HB)
                    pool.tensor_tensor(X[:, part, :], X[:, part, :],
                                       BIAS[:, :].unsqueeze(1).broadcast_to([T, HB, D]),
                                       ALU.add).then_inc(xb_ready, 1)

            with pool.Fori(0, GROUPS - 1) as i:
                group(i, True)
            group(GROUPS - 1, False)

        @block.tensor
        def _(pe):
            def graph_u(s, g):
                first = s == 0 and isinstance(g, int) and g == 0
                if not first:
                    pe.wait_ge(h0_ready, STREAMS * g + s)
                for n in range(HB):
                    if first:
                        pe.wait_ge(h0_first, n + 1)
                    mm = pe.matmul(as_batches(bank(s, 2 + n // PACK))[:, n % PACK, :],
                                   H0[:, s * HB + n, :], ADJ[:, :], start=True, stop=True)
                    if n % PACK == PACK - 1:
                        mm.then_inc(u_mm, 1)

            def graph_z(s, g, after_transpose):
                for n in range(HBANKS):
                    pe.wait_ge(u_sb, 2 * HBANKS * g + s * HBANKS + n + 1)
                    if after_transpose:
                        pe.wait_ge(x2_ready, 2 * HBANKS * (g - 1) + s * HBANKS + n + 1)
                    pe.matmul(bank(s, n), WG0[:, :], U[:, s, 512 * n:512 * n + 512],
                              start=True, stop=True).then_inc(z_mm, 1)

            def graph_y(s, g):
                for n in range(HB):
                    if n % PACK == 0:
                        pe.wait_ge(h1_ready, 2 * HBANKS * g + s * HBANKS + n // PACK + 1)
                    mm = pe.matmul(as_batches(bank(s, 2 + n // PACK))[:, n % PACK, :],
                                   Z[:, s, T * n:T * n + T], WG1[:, :], start=True, stop=True)
                    if n % PACK == PACK - 1:
                        mm.then_inc(y_mm, 1)

            def graph_v(s, g):
                for n in range(HB):
                    if n % PACK == 0:
                        pe.wait_ge(y_sb, 2 * HBANKS * g + s * HBANKS + n // PACK + 1)
                    mm = pe.matmul(as_batches(bank(s, n // PACK))[:, n % PACK, :],
                                   Y[:, s, D * n:D * n + D], ADJ[:, :], start=True, stop=True)
                    if n % PACK == PACK - 1:
                        mm.then_inc(v_mm, 1)

            def unit(k, i, last):
                p, s, j, w0, nw, gates = UNITS[k]
                prev = last_unit(k, s)
                n = nw * HB
                if prev is None:
                    pe.wait_ge(h_high, 2 * HBANKS * i + HBANKS * (s + 1))
                    pe.wait_ge(h_low, 2 * HBANKS * i + HBANKS * (s + 1))
                if s == 0 and j == 0 and w0 == 0 and isinstance(i, int) and i == 0:
                    pe.wait_ge(split_w, 4 * p - 2)
                if last and k in OUT_BEFORE:
                    pe.wait_ge(out_ready, len(CHUNKS) * (i - 1) + OUT_BEFORE[k])
                x_high, x_low = windows(HH, s, p, j, w0, nw), windows(HL, s, p, j, w0, nw)
                for m, q in enumerate(gates):
                    for what, b in LAST_AT.get((k, m), ()) if last else ():
                        last_piece(what, b, i - 1, k)
                    if j == 0 and p > 1 and m == 0:
                        pe.wait_ge(lstm_step, STEPS * i + STEPS_BEFORE[prev] + STEPS_OF[prev])
                    if prev is not None:
                        read = UNITS[prev][5].index(q) if q in UNITS[prev][5] else 0
                        pe.wait_ge(gate_act, GATES * i + GATES_BEFORE[prev] + read + 1)
                    dst = bank(s, q)[:, 0:n].rearrange("p (w b) -> p w b", b=HB)
                    cols = slice(q * D, q * D + D)
                    pe.matmul(dst, WIH[:, p - 1, cols], x_high, start=True, stop=False)
                    pe.matmul(dst, WIL[:, p - 1, cols], x_high, start=False, stop=False)
                    if j == 0 and p > 1 and m == 0:
                        pe.wait_ge(h_out, len(UNITS) * i + prev + 1)
                    mm = pe.matmul(dst, WIH[:, p - 1, cols], x_low, start=False, stop=(j == 0))
                    if j == 0:
                        mm.then_inc(gate_mm, 1)
                if j > 0:
                    pe.wait_ge(lstm_step, STEPS * i + STEPS_BEFORE[prev] + STEPS_OF[prev])
                    for q in gates:
                        dst = bank(s, q)[:, 0:n]
                        cols = slice(q * D, q * D + D)
                        pe.matmul(dst, WHH[:, p - 2, cols], SH[:, s, 0:n], start=False, stop=False)
                        pe.matmul(dst, WHL[:, p - 2, cols], SH[:, s, 0:n], start=False, stop=False)
                        if q == gates[0]:
                            pe.wait_ge(h_out, len(UNITS) * i + prev + 1)
                        pe.matmul(dst, WHH[:, p - 2, cols], SL[:, s, 0:n], start=False,
                                  stop=True).then_inc(gate_mm, 1)
                for what, b in LAST_AT.get((k, len(gates)), ()) if last else ():
                    last_piece(what, b, i - 1, k)

            def transpose_h(s, i):
                pe.wait_ge(lstm_step, STEPS * i + STEPS_BEFORE[LAST_OF[s] + 1])
                for n in range(HB):
                    dst = as_batches(bank(s, n // PACK))[:, n % PACK, :]
                    pe.matmul(dst, HH[:, s, :, n], IDENTR[:, :], start=True, stop=False)
                    if n == 0:
                        pe.wait_ge(h_out, len(UNITS) * i + LAST_OF[s] + 1)
                    mm = pe.matmul(dst, HL[:, s, :, n], IDENTR[:, :], start=False, stop=True)
                    if n % PACK == PACK - 1:
                        mm.then_inc(t_mm, 1)

            def last_uk(g, n, ps):
                if n < HB:
                    pe.wait_ge(h3_first, HB * g + n + 1)
                elif n == HB:
                    pe.wait_ge(h3_second, g + 1)
                pe.matmul(ps[:, 0:ADJ_PARTS * T], H3[:, n, :], ADJ3[:, :, :].rearrange("p k t -> p (k t)"),
                          start=True, stop=True).then_inc(uk_mm, 1)

            def last_out(g, n, ps):
                c, first, last = chunk_of(n)
                pe.wait_ge(uk_sb, G * g + n + 1)
                for k in range(ADJ_PARTS):
                    mm = pe.matmul(as_batches(ps)[:, n - CHUNKS[c][0], :], UK[:, n % 4, k * T:(k + 1) * T],
                                   WL1[:, k, :], start=(k == 0), stop=(k == ADJ_PARTS - 1))
                if last:
                    mm.then_inc(out_mm, 1)

            def last_piece(what, n, g, k):
                c, first, last = chunk_of(n)
                if what == ADJP:
                    if n in AFTER_F:
                        pe.wait_ge(gate_act, GATES * g + GATES + GATES_BEFORE[last_unit(k, 0)] + 3)
                    elif n:
                        pe.wait_ge(uk_sb, G * g + n)
                    last_uk(g, n, bank(0, F))
                else:
                    if n in AFTER_F:
                        pe.wait_ge(gate_act, GATES * g + GATES + GATES_BEFORE[last_unit(k, 1)] + 3)
                    elif first and n:
                        pe.wait_ge(out_ready, len(CHUNKS) * g + c)
                    last_out(g, n, bank(1, F))

            pe.wait_ge(w_adj, 3 * 16)
            pe.wait_ge(consts, 2)
            pe.matmul(bank(0, 0)[:, 0:T], ONES[:, :], ADJ[:, :], start=True, stop=True).then_inc(rowsum_mm, 1)
            for s in range(STREAMS):
                graph_u(s, 0)
            pe.wait_ge(bias_ready, 2)
            pe.wait_ge(w_gcn, 4 * 16)
            for s in range(STREAMS):
                graph_z(s, 0, False)
            for s in range(STREAMS):
                graph_y(s, 0)
            for s in range(STREAMS):
                graph_v(s, 0)

            def units(i, last):
                for k in range(len(UNITS)):
                    unit(k, i, last)

            def next_graph(i):
                pe.wait_ge(gate_act, GATES * i + GATES_BEFORE[LAST_OF[0]] + len(LATER_STEP))
                graph_u(0, i + 1)
                transpose_h(0, i)
                pe.wait_ge(gate_act, GATES * i + GATES)
                graph_u(1, i + 1)
                transpose_h(1, i)
                graph_z(0, i + 1, True)
                graph_z(1, i + 1, True)
                for s in range(STREAMS):
                    graph_y(s, i + 1)
                for s in range(STREAMS):
                    graph_v(s, i + 1)

            units(0, False)
            pe.wait_ge(consts, 8)
            pe.wait_ge(w_late, 32)
            next_graph(0)
            with pe.Fori(1, GROUPS - 1) as i:
                units(i, True)
                next_graph(i)
            i = GROUPS - 1
            units(i, True)
            transpose_h(0, i)
            transpose_h(1, i)
            ring = [bank(0, 2), bank(0, 3), bank(1, 2), bank(1, 3)]
            out_ring = [bank(0, 0), bank(0, 1), bank(1, 0), bank(1, 1)]
            lag = 2
            for n in range(G + lag):
                if n < G:
                    last_uk(i, n, ring[n % 4])
                if n >= lag:
                    c, first, last = chunk_of(n - lag)
                    if first and c >= 4:
                        pe.wait_ge(out_ready, len(CHUNKS) * i + c - 3)
                    last_out(i, n - lag, out_ring[c % 4])

        @block.scalar
        def _(act):
            def relu_h0(s, g):
                act.wait_ge(norm1, G * g + HB * s)
                part = H0[:, s * HB:(s + 1) * HB, :]
                act.activation(part, part, ACT.Relu).then_inc(h0_ready, 1)

            def copy_u(s, g):
                for n in range(HBANKS):
                    act.wait_ge(u_mm, 2 * HBANKS * g + s * HBANKS + n + 1)
                    act.activation(U[:, s, 512 * n:512 * n + 512], bank(s, 2 + n), ACT.Copy).then_inc(u_sb, 1)

            def relu_z(s, g):
                for n in range(HBANKS):
                    act.wait_ge(z_sb, 2 * HBANKS * g + s * HBANKS + n + 1)
                    part = Z[:, s, 512 * n:512 * n + 512]
                    act.activation(part, part, ACT.Relu).then_inc(h1_ready, 1)

            def high_h(s, g):
                for n in range(HBANKS):
                    act.wait_ge(v_mm, 2 * HBANKS * g + s * HBANKS + n + 1)
                    act.activation(HH[:, s, :, n * PACK:(n + 1) * PACK].rearrange("p t b -> p b t"),
                                   as_batches(bank(s, n)), ACT.Relu).then_inc(h_high, 1)

            def norm_relu_h3(i):
                act.wait_ge(shift2, i + 1)
                for b in range(HB):
                    act.activation(H3[:, b, :], X[:, i * G + b, :], ACT.Relu,
                                   bias=SHIFT2[:, b:b + 1], scale=RS2[:, b:b + 1]).then_inc(h3_first, 1)


            def copy_uk(g, n, ps):
                act.wait_ge(uk_mm, G * g + n + 1)
                act.activation(UK[:, n % 4, :], ps[:, 0:ADJ_PARTS * T], ACT.Copy).then_inc(uk_sb, 1)

            act.wait_ge(consts, 2)
            act.activation(TC[:, 0, 0:G], NHALF[:, :], ACT.Sigmoid)
            act.wait_ge(shift1, 1)
            for b in range(HB):
                act.activation(H0[:, b, :], X[:, b, :], ACT.Relu, bias=SHIFT1[:, b:b + 1],
                               scale=RS1[:, b:b + 1]).then_inc(h0_first, 1)
            relu_h0(1, 0)
            for part in (copy_u, relu_z, high_h):
                part(0, 0)
                part(1, 0)
            act.wait_ge(bias_ready, 1)

            def unit(k, i, last):
                p, s, j, w0, nw, gates = UNITS[k]
                prev = last_unit(k, s)
                n = nw * HB
                if p == 1 and prev is not None:
                    act.wait_ge(lstm_step, STEPS * i + STEPS_BEFORE[prev] + STEPS_OF[prev] - 1)
                for m, q in enumerate(gates):
                    for what, b in LAST_AT.get((k, m), ()) if last else ():
                        if what == ADJP:
                            copy_uk(i - 1, b, bank(0, F))
                    act.wait_ge(gate_mm, GATES * i + GATES_BEFORE[k] + m + 1)
                    act.activation(GT[:, s, q, 0:n], bank(s, q)[:, 0:n],
                                   ACT.Tanh if q == C else ACT.Sigmoid,
                                   bias=BG[:, 4 * (p - 1) + q:4 * (p - 1) + q + 1]).then_inc(gate_act, 1)
                for what, b in LAST_AT.get((k, len(gates)), ()) if last else ():
                    if what == ADJP:
                        copy_uk(i - 1, b, bank(0, F))
                act.wait_ge(cell_ready, len(UNITS) * i + k + 1)
                act.activation(TC[:, s, 0:n], CS[:, s, 0:n], ACT.Tanh).then_inc(tanh_ready, 1)

            def units(i, more, last):
                for k in range(len(UNITS)):
                    unit(k, i, last)
                    if more and k in LN_RELU_AT:
                        relu_h0(LN_RELU_AT[k], i + 1)

            def next_graph(i):
                for part in (copy_u, relu_z):
                    part(0, i + 1)
                    part(1, i + 1)
                norm_relu_h3(i)
                high_h(0, i + 1)
                high_h(1, i + 1)

            units(0, True, False)
            next_graph(0)
            with act.Fori(1, GROUPS - 1) as i:
                units(i, True, True)
                next_graph(i)
            i = GROUPS - 1
            units(i, False, True)
            norm_relu_h3(i)
            ring = [bank(0, 2), bank(0, 3), bank(1, 2), bank(1, 3)]
            for n in range(G):
                copy_uk(i, n, ring[n % 4])

        @block.vector
        def _(dve):
            def stats1(g, batches):
                for b in batches:
                    dve.bn_stats(ST1[:, b, :], X[:, g * G + b, :]).then_inc(bn1, 1)

            def combine(st, done, count, before, mean, ve, var, lo, hi, sign=1):
                diff, total, spread, square, both = (LN[:, n, lo:hi] for n in range(5))
                dve.wait_ge(done, count)
                dve.tensor_tensor(diff, st[:, lo:hi, 1], st[:, lo:hi, 4], ALU.subtract).then_inc(ln_step, 1)
                dve.tensor_tensor(total, st[:, lo:hi, 1], st[:, lo:hi, 4], ALU.add).then_inc(ln_step, 1)
                dve.tensor_tensor(spread, st[:, lo:hi, 2], st[:, lo:hi, 5], ALU.add).then_inc(ln_step, 1)
                dve.wait_ge(ln_step, before + 1)
                dve.tensor_tensor(square, diff, diff, ALU.mult).then_inc(ln_step, 1)
                dve.wait_ge(ln_step, before + 2)
                dve.tensor_scalar(mean[:, lo:hi], total, sign * 0.5, None, ALU.mult).then_inc(var, 1)
                dve.wait_ge(ln_step, before + 4)
                dve.scalar_tensor_tensor(out=both, in0=square, scalar=D / 4, in1=spread,
                                         op0=ALU.mult, op1=ALU.add).then_inc(ln_step, 1)
                dve.wait_ge(ln_step, before + 5)
                dve.tensor_scalar(ve[:, lo:hi], both, 1 / D, EPS, ALU.mult, ALU.add).then_inc(var, 1)

            def norm_h0(g, ready, batches):
                dve.wait_ge(rs1, ready)
                for b in batches:
                    dve.tensor_scalar(H0[:, b, :], X[:, g * G + b, :], MINUS1[:, b:b + 1], RS1[:, b:b + 1],
                                      ALU.add, ALU.mult).then_inc(norm1, 1)

            def bias_z(s, g):
                for n in range(HBANKS):
                    dve.wait_ge(z_mm, 2 * HBANKS * g + s * HBANKS + n + 1)
                    dve.tensor_tensor(as_batches(Z[:, s, 512 * n:512 * n + 512]), as_batches(bank(s, n)),
                                      BG0T[:, :].unsqueeze(1).broadcast_to([128, PACK, T]),
                                      ALU.add).then_inc(z_sb, 1)

            def bias_y(s, g):
                for n in range(HBANKS):
                    dve.wait_ge(y_mm, 2 * HBANKS * g + s * HBANKS + n + 1)
                    dve.tensor_tensor(as_batches(Y[:, s, 512 * n:512 * n + 512]), as_batches(bank(s, 2 + n)),
                                      BG1[:, :].unsqueeze(1).broadcast_to([128, PACK, D]),
                                      ALU.add).then_inc(y_sb, 1)

            def low_h(s, g):
                for n in range(HBANKS):
                    dve.wait_ge(h_high, 2 * HBANKS * g + s * HBANKS + n + 1)
                    part = slice(n * PACK, (n + 1) * PACK)
                    dve.scalar_tensor_tensor(out=HL[:, s, :, part].rearrange("p t b -> p b t"),
                                             in0=as_batches(bank(s, n)), scalar=0.0,
                                             in1=HH[:, s, :, part].rearrange("p t b -> p b t").bitcast(F32),
                                             op0=ALU.max, op1=ALU.subtract).then_inc(h_low, 1)

            def unit_cell(k, i):
                p, s, j, w0, nw, gates = UNITS[k]
                n = nw * HB
                done = GATES * i + GATES_BEFORE[k]
                steps = STEPS * i + STEPS_BEFORE[k]
                dve.wait_ge(gate_act, done + 2)
                if j == 0:
                    dve.tensor_tensor(CS[:, s, 0:n], GT[:, s, I, 0:n], GT[:, s, C, 0:n],
                                      ALU.mult).then_inc(cell_ready, 1)
                    return
                dve.tensor_tensor(IC[:, s, 0:n], GT[:, s, I, 0:n], GT[:, s, C, 0:n],
                                  ALU.mult).then_inc(lstm_step, 1)
                dve.wait_ge(gate_act, done + 3)
                dve.tensor_tensor(CS[:, s, 0:n], GT[:, s, F, 0:n], CS[:, s, 0:n],
                                  ALU.mult).then_inc(lstm_step, 1)
                dve.wait_ge(lstm_step, steps + 2)
                dve.tensor_tensor(CS[:, s, 0:n], IC[:, s, 0:n], CS[:, s, 0:n],
                                  ALU.add).then_inc(cell_ready, 1)

            def unit_hidden(k, i):
                p, s, j, w0, nw, gates = UNITS[k]
                n = nw * HB
                steps = STEPS * i + STEPS_BEFORE[k] + STEPS_OF[k]
                dve.wait_ge(tanh_ready, len(UNITS) * i + k + 1)
                dve.tensor_tensor(HT[:, s, 0:n], GT[:, s, O, 0:n], TC[:, s, 0:n],
                                  ALU.mult).then_inc(lstm_step, 1)
                if j == p - 1:
                    high, low = windows(HH, s, p, j, w0, nw), windows(HL, s, p, j, w0, nw)
                    full = HT[:, s, 0:n].rearrange("p (w b) -> p w b", b=HB)
                else:
                    high, low, full = SH[:, s, 0:n], SL[:, s, 0:n], HT[:, s, 0:n]
                dve.wait_ge(lstm_step, steps - 1)
                dve.tensor_copy(high, full).then_inc(lstm_step, 1)
                dve.wait_ge(lstm_step, steps)
                dve.tensor_tensor(low, full, high.bitcast(F32), ALU.subtract).then_inc(h_out, 1)

            def add_x(s, i):
                for n in range(HBANKS):
                    dve.wait_ge(t_mm, 2 * HBANKS * i + s * HBANKS + n + 1)
                    part = bass.ds(i * G + s * HB + n * PACK, PACK)
                    dve.tensor_tensor(X[:, part, :], as_batches(bank(s, n)), X[:, part, :],
                                      ALU.add).then_inc(x2_ready, 1)

            def stats2(s, i):
                wait_apart(dve, x2_ready, 2 * HBANKS * i + HBANKS * (s + 1), x_first, 16)
                for b in range(s * HB, s * HB + HB):
                    dve.bn_stats(ST2[:, b, :], X[:, i * G + b, :]).then_inc(bn2, 1)

            def combine2(s, i, more):
                combine(ST2, bn2, G * i + HB * (s + 1), COMBINE * (3 * i + s + (3 if more else 2)),
                        MINUS2, VE2, var2, s * HB, s * HB + HB, sign=-1)

            def norm_h3(i):
                dve.wait_ge(rs2, STREAMS * i + 2)
                for b in range(HB, G):
                    dve.tensor_scalar(H3[:, b, :], X[:, i * G + b, :], MINUS2[:, b:b + 1], RS2[:, b:b + 1],
                                      ALU.add, ALU.mult).then_inc(norm2, 1)
                wait_apart(dve, norm2, HB * i + HB, x_first, 16)
                dve.tensor_scalar(H3[:, HB:G, :], H3[:, HB:G, :], 0.0, None, ALU.max).then_inc(h3_second, 1)

            def add_out(g, c, ps):
                first, size = CHUNKS[c]
                dve.wait_ge(out_mm, len(CHUNKS) * g + c + 1)
                dve.wait_ge(xb_ready, STREAMS * g + (first + size - 1) // HB + 1)
                part = bass.ds(g * G + first, size)
                dve.tensor_tensor(X[:, part, :], as_batches(ps)[:, 0:size, :], X[:, part, :],
                                  ALU.add).then_inc(out_ready, 1)

            for s in range(STREAMS):
                dve.wait_ge((x_first, x_second)[s], 16)
                stats1(0, range(HB * s, HB * s + HB))
                combine(ST1, bn1, HB * s + HB, COMBINE * s, MINUS1, VE1, var1, HB * s, HB * s + HB, sign=-1)
            norm_h0(0, 2, range(HB, G))
            dve.wait_ge(w_adj, 3 * 16)
            dve.wait_ge(w_gcn, 4 * 16)
            dve.tensor_tensor(BG[:, :], BI[:, :], BH[:, :], ALU.add).then_inc(bias_ready, 1)
            dve.wait_ge(rowsum_mm, 1)
            dve.tensor_scalar(BG0T[:, :], bank(0, 0)[:, 0:T], BG0[:, 0:1], None, ALU.mult).then_inc(bias_ready, 1)
            dve.wait_ge(bias_ready, 2)
            for part in (bias_z, bias_y, low_h):
                part(0, 0)
                part(1, 0)
            dve.wait_ge(x_rest, 16 * (GROUPS - 1))

            def units(i, more, last):
                for k in range(len(UNITS)):
                    if last and k in CHUNK_AHEAD:
                        add_out(i - 1, CHUNK_AHEAD[k], bank(1, F))
                    unit_cell(k, i)
                    if last and k in CHUNK_AFTER:
                        add_out(i - 1, CHUNK_AFTER[k], bank(1, F))
                    if more and k in LN_STATS_AT:
                        stats1(i + 1, LN_STATS_AT[k])
                    if more and k == LN_COMBINE_AT:
                        combine(ST1, bn1, G * i + 2 * G, COMBINE * (3 * i + 2), MINUS1, VE1, var1, 0, G, sign=-1)
                    if more and k in LN_APPLY_AT:
                        norm_h0(i + 1, i + 3, LN_APPLY_AT[k])
                    unit_hidden(k, i)
                    if last and k == 2:
                        norm_h3(i - 1)

            def next_graph(i):
                add_x(0, i)
                stats2(0, i)
                add_x(1, i)
                bias_z(0, i + 1)
                combine2(0, i, True)
                bias_z(1, i + 1)
                bias_y(0, i + 1)
                bias_y(1, i + 1)
                stats2(1, i)
                low_h(0, i + 1)
                combine2(1, i, True)
                low_h(1, i + 1)

            units(0, True, False)
            next_graph(0)
            with dve.Fori(1, GROUPS - 1) as i:
                units(i, True, True)
                next_graph(i)
            i = GROUPS - 1
            units(i, False, True)
            add_x(0, i)
            stats2(0, i)
            combine2(0, i, False)
            add_x(1, i)
            stats2(1, i)
            combine2(1, i, False)
            norm_h3(i)
            out_ring = [bank(0, 0), bank(0, 1), bank(1, 0), bank(1, 1)]
            for c in range(len(CHUNKS)):
                add_out(i, c, out_ring[c % 4])


def kernel(**inputs):
    import numpy as np
    import concourse.bacc as bacc
    from concourse import mybir as _mybir
    from concourse.bass_utils import run_bass_kernel_spmd

    a = {k: np.asarray(v) for k, v in inputs.items()}

    def gates_t(w):
        return w.transpose(2, 0, 1)

    laid_out = {
        "x_tbd": a["x"].transpose(1, 0, 2),
        "adj_t": a["adj"].T,
        "wg0": a["L0_gnn_Wg0"],
        "bg0_col": a["L0_gnn_bg0"].reshape(D, 1),
        "wg1": a["L0_gnn_Wg1"],
        "bg1": a["L0_gnn_bg1"],
        "wih_t": gates_t(a["L0_gnn_Wih"]),
        "whh_t": gates_t(a["L0_gnn_Whh"][1:]),
        "bih_t": a["L0_gnn_bih"].reshape(16, D).T,
        "bhh_t": a["L0_gnn_bhh"].reshape(16, D).T,
        "w_l1": a["L1_gnn_W"].transpose(1, 0, 2),
        "bias": a["L1_gnn_bias"],
    }
    nc = bacc.Bacc("TRN2", target_bir_lowering=False, num_devices=1)
    arrays, args = {}, []
    for name, v in laid_out.items():
        v = np.ascontiguousarray(v)
        arrays[name] = v
        args.append(nc.dram_tensor(name, v.shape, _mybir.dt.from_np(v.dtype), kind="ExternalInput").ap())
    args.append(nc.dram_tensor("out_tbd", (T, B, D), _mybir.dt.float32, kind="ExternalOutput").ap())
    program(nc, *args)
    r = run_bass_kernel_spmd(nc, [arrays], core_ids=[0])
    return np.ascontiguousarray(r.results[0]["out_tbd"].transpose(1, 0, 2))
```

```python
from collections import namedtuple
from contextlib import ExitStack

import concourse.bass as bass
from concourse import mybir

F32 = mybir.dt.float32
F32R = mybir.dt.float32r
ALU = mybir.AluOpType
ACT = mybir.ActivationFunctionType

B, T, D = 64, 128, 128
G = 16
GROUPS = B // G
HB = G // 2
STREAMS = 2
PACK = 512 // T
QUARTERS = 4
HBANKS = HB // PACK
EPS = 1e-5
ADJ_PARTS = 3

I, F, C, O = range(4)
FIRST_STEP = (I, C, O)
LATER_STEP = (I, C, F, O)
F_READ = LATER_STEP.index(F) + 1
SKIPS = (1, 2, 3, 4)


def lstm_units():
    units = []
    for p in SKIPS:
        chunks = max(1, (T // p) * HB // 512)
        nw = (T // p) // chunks
        for c in range(chunks):
            for j in range(p):
                for s in range(STREAMS):
                    units.append((p, s, j, c * nw, nw, FIRST_STEP if j == 0 else LATER_STEP))
    return units


UNITS = lstm_units()
GATES_BEFORE = [sum(len(u[5]) for u in UNITS[:k]) for k in range(len(UNITS) + 1)]
GATES = GATES_BEFORE[-1]
STEPS_OF = [2 if u[5] == FIRST_STEP else 4 for u in UNITS]
STEPS_BEFORE = [sum(STEPS_OF[:k]) for k in range(len(UNITS) + 1)]
STEPS = STEPS_BEFORE[-1]


def last_unit(k, s):
    return next((n for n in range(k - 1, -1, -1) if UNITS[n][1] == s), None)


LAST_OF = [last_unit(len(UNITS), s) for s in range(STREAMS)]

ADJP, OUTP = "adj", "out"
Plan = namedtuple("Plan", [
    "at",
    "after_f",
    "chunks",
    "read_after",
    "read_ahead",
    "out_before",
])


def both(n):
    return (ADJP, n), (OUTP, n - 1)


START = {(1, 1): ((ADJP, 0),), (2, 0): both(1), (2, 1): both(2), (2, 2): both(3),
         (3, 0): both(4), (3, 1): both(5), (3, 2): both(6)}
STEADY = Plan(
    at={**START, (4, 0): both(7), (4, 1): both(8), (4, 2): both(9), (5, 0): both(10), (5, 1): ((OUTP, 10),),
        (7, 4): ((ADJP, 11),), (9, 0): both(12), (10, 1): ((OUTP, 12),),
        (13, 4): ((ADJP, 13),), (15, 0): both(14), (15, 2): both(15), (16, 1): ((OUTP, 15),)},
    after_f=(11, 13), chunks=((0, 3), (3, 3), (6, 3), (9, 2), (11, 2), (13, 3)),
    read_after={2: 0, 3: 1, 4: 2, 5: 3}, read_ahead={10: 4, 16: 5}, out_before={7: 4, 11: 5, 17: 6})
LATE = Plan(
    at={**START, (4, 0): ((OUTP, 6),), (7, 4): ((ADJP, 7),), (9, 0): both(8), (10, 1): ((OUTP, 8),),
        (13, 4): ((ADJP, 9),), (15, 0): both(10), (15, 2): both(11), (16, 1): ((OUTP, 11),)},
    after_f=(7, 9), chunks=((0, 3), (3, 3), (6, 1), (7, 2), (9, 3), (12, 4)),
    read_after={2: 0, 3: 1, 4: 2}, read_ahead={10: 3, 16: 4}, out_before={7: 3, 11: 4, 17: 5})
CHUNKS = len(STEADY.chunks)
TAIL = range(LATE.chunks[-1][0], G)

NORM_AT, SPLIT_AT = 0, 2
CELL_EARLY = (1, 2, 15)


def chunk_of(plan, n):
    c = next(c for c, (first, size) in enumerate(plan.chunks) if first <= n < first + size)
    return c, n == plan.chunks[c][0], n == sum(plan.chunks[c]) - 1


LN_STATS_AT = {4 + k: range(3 * k, min(3 * k + 3, G)) for k in range(6)}
LN_COMBINE_AT = 10
LN_APPLY_AT = {12 + k: (2 * k, 2 * k + 1) for k in range(G // 2)}
LN_RELU_AT = {15: 0, 19: 1}


def program(nc, x_tbd, adj_t, wg0, bg0_col, wg1, bg1, wih_t, whh_t, bih_t, bhh_t, w_l1, bias, out_tbd):
    with ExitStack() as ctx:
        def sb(name, shape, dt=F32):
            return ctx.enter_context(nc.sbuf_tensor(name, shape, dt))

        def sem(name):
            return ctx.enter_context(nc.semaphore(name))

        X = sb("X", [T, B, D])
        H0 = sb("H0", [T, G, D])
        H3 = sb("H3", [T, G, D])
        H3H = sb("H3H", [T, HB, D], F32R)
        H3L = sb("H3L", [T, HB, D], F32R)
        U = sb("U", [128, STREAMS, HB * T])
        Z = sb("Z", [128, STREAMS, HB * T])
        Y = sb("Y", [T, STREAMS, HB * D])
        UK = sb("UK", [128, 4, ADJ_PARTS * T])
        HH = sb("HH", [128, STREAMS, T, HB], F32R)
        HL = sb("HL", [128, STREAMS, T, HB], F32R)
        SH = sb("SH", [128, STREAMS, 512], F32R)
        SL = sb("SL", [128, STREAMS, 512], F32R)
        GT = sb("GT", [128, STREAMS, 4, 512])
        CS = sb("CS", [128, STREAMS, 512])
        IC = sb("IC", [128, STREAMS, 512])
        TC = sb("TC", [128, STREAMS, 512])
        HT = sb("HT", [128, STREAMS, 512])
        WI = sb("WI", [D, 4, 4 * D])
        WH = sb("WH", [D, 3, 4 * D])
        WIH = sb("WIH", [D, 4, 4 * D], F32R)
        WIL = sb("WIL", [D, 4, 4 * D], F32R)
        WHH = sb("WHH", [D, 3, 4 * D], F32R)
        WHL = sb("WHL", [D, 3, 4 * D], F32R)
        ADJ = sb("ADJ", [T, T])
        ADJ3 = sb("ADJ3", [T, ADJ_PARTS, T])
        ADJ3H = sb("ADJ3H", [T, ADJ_PARTS, T], F32R)
        ADJ3L = sb("ADJ3L", [T, ADJ_PARTS, T], F32R)
        WG0 = sb("WG0", [D, D])
        WG1 = sb("WG1", [D, D])
        WL1 = sb("WL1", [D, ADJ_PARTS, D])
        BG0 = sb("BG0", [D, 1])
        BG0T = sb("BG0T", [D, T])
        BG1 = sb("BG1", [T, D])
        BIAS = sb("BIAS", [T, D])
        BI = sb("BI", [D, 16])
        BH = sb("BH", [D, 16])
        BG = sb("BG", [D, 16])
        ONES = sb("ONES", [T, D])
        IDENT = sb("IDENT", [128, 128])
        IDENTR = sb("IDENTR", [128, 128], F32R)
        ST1 = sb("ST1", [T, G, 6])
        MINUS1 = sb("MINUS1", [T, G])
        SHIFT1 = sb("SHIFT1", [T, G])
        VE1 = sb("VE1", [T, G])
        RS1 = sb("RS1", [T, G])
        ST2 = sb("ST2", [T, G, 6])
        MINUS2 = sb("MINUS2", [T, G])
        SHIFT2 = sb("SHIFT2", [T, HB])
        LN = sb("LN", [T, 5, G])
        VE2 = sb("VE2", [T, G])
        RS2 = sb("RS2", [T, G])
        NHALF = sb("NHALF", [T, G])
        PS = ctx.enter_context(nc.psum_tensor("PS", [128, 8, 512], F32))

        x_quarter = [sem(f"x_quarter{q}") for q in range(QUARTERS)]
        x_rest = sem("x_rest")
        w_adj = sem("w_adj")
        w_gcn = sem("w_gcn")
        w_lstm = sem("w_lstm")
        w_late = sem("w_late")
        consts = sem("consts")
        split_w = sem("split_w")
        bias_ready = sem("bias_ready")
        rowsum_mm = sem("rowsum_mm")
        bn1 = sem("bn1")
        ln_step = sem("ln_step")
        var1 = sem("var1")
        rs1 = sem("rs1")
        shift1 = sem("shift1")
        norm1 = sem("norm1")
        h0_first = sem("h0_first")
        h0_ready = sem("h0_ready")
        u_mm = sem("u_mm")
        u_sb = sem("u_sb")
        z_mm = sem("z_mm")
        z_sb = sem("z_sb")
        h1_ready = sem("h1_ready")
        y_mm = sem("y_mm")
        y_sb = sem("y_sb")
        out_ready = sem("out_ready")
        v_mm = sem("v_mm")
        h_high = sem("h_high")
        h_low = sem("h_low")
        gate_mm = sem("gate_mm")
        gate_act = sem("gate_act")
        lstm_step = sem("lstm_step")
        cell_ready = sem("cell_ready")
        tanh_ready = sem("tanh_ready")
        h_out = sem("h_out")
        t_mm = sem("t_mm")
        x2_ready = sem("x2_ready")
        bn2 = sem("bn2")
        var2 = sem("var2")
        rs2 = sem("rs2")
        shift2 = sem("shift2")
        norm2 = sem("norm2")
        h3_first = sem("h3_first")
        h3_high = sem("h3_high")
        h3_second = sem("h3_second")
        xb_ready = sem("xb_ready")
        uk_mm = sem("uk_mm")
        uk_sb = sem("uk_sb")
        out_mm = sem("out_mm")
        stored = sem("stored")

        COMBINE = 5

        def bank(s, n):
            return PS[:, 4 * s + n, :]

        def as_batches(ap):
            return ap.rearrange("p (b t) -> p b t", b=PACK)

        def windows(h, s, p, j, w0, nw):
            first = p * w0 + j
            return h[:, s, first:first + p * (nw - 1) + 1:p, :]

        def wait_apart(eng, sem, count, met, met_count):
            count = count if isinstance(count, int) else eng.snap(count)
            eng.wait_ge(met, met_count)
            eng.wait_ge(sem, count)

        block = ctx.enter_context(nc.Block())

        @block.sync
        def _(sp):
            for q in range(QUARTERS):
                part = slice(q * G // QUARTERS, (q + 1) * G // QUARTERS)
                sp.dma_start(X[:, part, :], x_tbd[:, part, :]).then_inc(x_quarter[q], 16)
                if q == 0:
                    sp.dma_start(ADJ[:, :], adj_t).then_inc(w_adj, 16)
            sp.dma_start(WG0[:, :], wg0).then_inc(w_gcn, 16)
            sp.dma_start(BG0[:, :], bg0_col).then_inc(w_gcn, 16)
            sp.dma_start(WG1[:, :], wg1).then_inc(w_gcn, 16)
            sp.dma_start(BG1[:, :], bg1.rearrange("(a n) -> a n", a=1).broadcast_to([T, D])).then_inc(w_gcn, 16)
            sp.dma_start(BI[:, :], bih_t).then_inc(w_gcn, 16)
            sp.dma_start(BH[:, :], bhh_t).then_inc(w_gcn, 16)
            sp.dma_start(WI[:, :, :], wih_t).then_inc(w_lstm, 16)
            sp.dma_start(WH[:, :, :], whh_t).then_inc(w_lstm, 16)
            sp.dma_start(WL1[:, :, :], w_l1).then_inc(w_late, 16)
            sp.dma_start(BIAS[:, :], bias.rearrange("(a n) -> a n", a=1).broadcast_to([T, D])).then_inc(w_late, 16)
            for g in range(1, GROUPS):
                sp.dma_start(X[:, g * G:(g + 1) * G, :], x_tbd[:, g * G:(g + 1) * G, :]).then_inc(x_rest, 16)

            def store(i, plan):
                for c, (first, size) in enumerate(plan.chunks):
                    sp.wait_ge(out_ready, CHUNKS * i + c + 1)
                    part = bass.ds(i * G + first, size)
                    sp.dma_start(out_tbd[:, part, :], X[:, part, :]).then_inc(stored, 16)

            with sp.Fori(0, GROUPS - 2) as i:
                store(i, STEADY)
            store(GROUPS - 2, LATE)
            store(GROUPS - 1, STEADY)
            sp.wait_ge(stored, 16 * GROUPS * CHUNKS)

        @block.gpsimd
        def _(pool):
            pool.memset(ONES[:, :], 1.0).then_inc(consts, 1)
            pool.memset(NHALF[:, :], -0.5).then_inc(consts, 1)

            def rstd(ve, var, count, rs, done, lo, hi):
                pool.wait_ge(var, count)
                pool.tensor_tensor(rs[:, lo:hi], ve[:, lo:hi], NHALF[:, lo:hi], ALU.pow).then_inc(done, 1)

            pool.wait_ge(consts, 2)
            for q in range(QUARTERS):
                part = slice(q * G // QUARTERS, (q + 1) * G // QUARTERS)
                rstd(VE1, var1, 2 * q + 2, RS1, rs1, part.start, part.stop)
                pool.wait_ge(rs1, q + 1)
                pool.tensor_tensor(SHIFT1[:, part], MINUS1[:, part], RS1[:, part], ALU.mult).then_inc(shift1, 1)

            pool.wait_ge(w_lstm, 32)
            done = 0
            for p in range(4):
                pairs = [(WI[:, p, :], WIH[:, p, :], WIL[:, p, :])]
                if p:
                    pairs.append((WH[:, p - 1, :], WHH[:, p - 1, :], WHL[:, p - 1, :]))
                for w, high, low in pairs:
                    pool.tensor_copy(high, w).then_inc(split_w, 1)
                    done += 1
                    pool.wait_ge(split_w, done)
                    pool.tensor_tensor(low, w, high.bitcast(F32), ALU.subtract).then_inc(split_w, 1)
                    done += 1

            pool.memset(IDENT[:, :], 0.0).then_inc(consts, 1)
            pool.wait_ge(consts, 3)
            pool.affine_select(out=IDENT[:, :], in_=IDENT[:, :], compare_op=ALU.not_equal, fill=1.0,
                               base=0, pattern=[[-1, 128]], channel_multiplier=1).then_inc(consts, 1)
            pool.wait_ge(consts, 4)
            pool.tensor_copy(IDENTR[:, :], IDENT[:, :]).then_inc(consts, 1)
            pool.wait_ge(w_adj, 16)
            for k, (op, sign) in enumerate(((ALU.is_equal, 1), (ALU.is_gt, 1), (ALU.is_gt, -1))):
                pool.affine_select(out=ADJ3[:, k, :], in_=ADJ[:, :], compare_op=op, fill=0.0,
                                   base=0, pattern=[[-sign, T]], channel_multiplier=sign).then_inc(consts, 1)
            pool.wait_ge(consts, 8)
            pool.tensor_copy(ADJ3H[:, :, :], ADJ3[:, :, :]).then_inc(consts, 1)
            pool.wait_ge(consts, 9)
            pool.tensor_tensor(ADJ3L[:, :, :], ADJ3[:, :, :], ADJ3H[:, :, :].bitcast(F32),
                               ALU.subtract).then_inc(consts, 1)
            pool.wait_ge(w_late, 32)

            def group(i, more):
                if more:
                    rstd(VE1, var1, 2 * (QUARTERS + i + 1), RS1, rs1, 0, G)
                for s in range(STREAMS):
                    rstd(VE2, var2, 2 * STREAMS * i + 2 * s + 2, RS2, rs2, HB * s, HB * s + HB)
                    if s == 0:
                        pool.wait_ge(rs2, STREAMS * i + 1)
                        pool.tensor_tensor(SHIFT2[:, :], MINUS2[:, 0:HB], RS2[:, 0:HB], ALU.mult).then_inc(shift2, 1)
                for s in range(STREAMS):
                    if s == 0:
                        pool.wait_ge(h3_first, HB * i + HB)
                    else:
                        pool.wait_ge(norm2, HB * i + HB)
                    part = bass.ds(i * G + s * HB, HB)
                    pool.tensor_tensor(X[:, part, :], X[:, part, :],
                                       BIAS[:, :].unsqueeze(1).broadcast_to([T, HB, D]),
                                       ALU.add).then_inc(xb_ready, 1)

            with pool.Fori(0, GROUPS - 1) as i:
                group(i, True)
            group(GROUPS - 1, False)

        @block.tensor
        def _(pe):
            def graph_u(s, g):
                first = isinstance(g, int) and g == 0
                if not first:
                    pe.wait_ge(h0_ready, STREAMS * (g - 1) + s + 1)
                for n in range(HB):
                    if first:
                        pe.wait_ge(h0_first, HB * s + n + 1)
                    mm = pe.matmul(as_batches(bank(s, 2 + n // PACK))[:, n % PACK, :],
                                   H0[:, s * HB + n, :], ADJ[:, :], start=True, stop=True)
                    if n % PACK == PACK - 1:
                        mm.then_inc(u_mm, 1)

            def graph_z(s, g, after_transpose):
                for n in range(HBANKS):
                    pe.wait_ge(u_sb, 2 * HBANKS * g + s * HBANKS + n + 1)
                    if after_transpose:
                        pe.wait_ge(x2_ready, 2 * HBANKS * (g - 1) + s * HBANKS + n + 1)
                    pe.matmul(bank(s, n), WG0[:, :], U[:, s, 512 * n:512 * n + 512],
                              start=True, stop=True).then_inc(z_mm, 1)

            def graph_y(s, g):
                for n in range(HB):
                    if n % PACK == 0:
                        pe.wait_ge(h1_ready, 2 * HBANKS * g + s * HBANKS + n // PACK + 1)
                    mm = pe.matmul(as_batches(bank(s, 2 + n // PACK))[:, n % PACK, :],
                                   Z[:, s, T * n:T * n + T], WG1[:, :], start=True, stop=True)
                    if n % PACK == PACK - 1:
                        mm.then_inc(y_mm, 1)

            def graph_v(s, g):
                for n in range(HB):
                    if n % PACK == 0:
                        pe.wait_ge(y_sb, 2 * HBANKS * g + s * HBANKS + n // PACK + 1)
                    mm = pe.matmul(as_batches(bank(s, n // PACK))[:, n % PACK, :],
                                   Y[:, s, D * n:D * n + D], ADJ[:, :], start=True, stop=True)
                    if n % PACK == PACK - 1:
                        mm.then_inc(v_mm, 1)

            def unit(k, i, plan):
                p, s, j, w0, nw, gates = UNITS[k]
                prev = last_unit(k, s)
                n = nw * HB
                if prev is None:
                    pe.wait_ge(h_high, 2 * HBANKS * i + HBANKS * (s + 1))
                    pe.wait_ge(h_low, 2 * HBANKS * i + HBANKS * (s + 1))
                if s == 0 and j == 0 and w0 == 0 and isinstance(i, int) and i == 0:
                    pe.wait_ge(split_w, 4 * p - 2)
                if plan and k in plan.out_before:
                    pe.wait_ge(out_ready, CHUNKS * (i - 1) + plan.out_before[k])
                x_high, x_low = windows(HH, s, p, j, w0, nw), windows(HL, s, p, j, w0, nw)
                for m, q in enumerate(gates):
                    for what, b in plan.at.get((k, m), ()) if plan else ():
                        last_piece(what, b, i - 1, k, plan)
                    if j == 0 and p > 1 and m == 0:
                        pe.wait_ge(lstm_step, STEPS * i + STEPS_BEFORE[prev] + STEPS_OF[prev])
                    if prev is not None:
                        read = UNITS[prev][5].index(q) if q in UNITS[prev][5] else 0
                        pe.wait_ge(gate_act, GATES * i + GATES_BEFORE[prev] + read + 1)
                    dst = bank(s, q)[:, 0:n].rearrange("p (w b) -> p w b", b=HB)
                    cols = slice(q * D, q * D + D)
                    pe.matmul(dst, WIH[:, p - 1, cols], x_high, start=True, stop=False)
                    pe.matmul(dst, WIL[:, p - 1, cols], x_high, start=False, stop=False)
                    if j == 0 and p > 1 and m == 0:
                        pe.wait_ge(h_out, len(UNITS) * i + prev + 1)
                    mm = pe.matmul(dst, WIH[:, p - 1, cols], x_low, start=False, stop=(j == 0))
                    if j == 0:
                        mm.then_inc(gate_mm, 1)
                if j > 0:
                    pe.wait_ge(lstm_step, STEPS * i + STEPS_BEFORE[prev] + STEPS_OF[prev])
                    for q in gates:
                        dst = bank(s, q)[:, 0:n]
                        cols = slice(q * D, q * D + D)
                        pe.matmul(dst, WHH[:, p - 2, cols], SH[:, s, 0:n], start=False, stop=False)
                        pe.matmul(dst, WHL[:, p - 2, cols], SH[:, s, 0:n], start=False, stop=False)
                        if q == gates[0]:
                            pe.wait_ge(h_out, len(UNITS) * i + prev + 1)
                        pe.matmul(dst, WHH[:, p - 2, cols], SL[:, s, 0:n], start=False,
                                  stop=True).then_inc(gate_mm, 1)
                for what, b in plan.at.get((k, len(gates)), ()) if plan else ():
                    last_piece(what, b, i - 1, k, plan)

            def transpose_h(s, i):
                pe.wait_ge(lstm_step, STEPS * i + STEPS_BEFORE[LAST_OF[s] + 1])
                for n in range(HB):
                    dst = as_batches(bank(s, n // PACK))[:, n % PACK, :]
                    pe.matmul(dst, HH[:, s, :, n], IDENTR[:, :], start=True, stop=False)
                    if n == 0:
                        pe.wait_ge(h_out, len(UNITS) * i + LAST_OF[s] + 1)
                    mm = pe.matmul(dst, HL[:, s, :, n], IDENTR[:, :], start=False, stop=True)
                    if n % PACK == PACK - 1:
                        mm.then_inc(t_mm, 1)

            def last_uk(g, n, ps):
                if n < HB:
                    pe.wait_ge(h3_first, HB * g + n + 1)
                elif n == HB:
                    pe.wait_ge(h3_second, g + 1)
                dst = ps[:, 0:ADJ_PARTS * T]
                adj, adj_high, adj_low = (a[:, :, :].rearrange("p k t -> p (k t)") for a in (ADJ3, ADJ3H, ADJ3L))
                if n < HB:
                    pe.matmul(dst, H3[:, n, :], adj, start=True, stop=True).then_inc(uk_mm, 1)
                else:
                    pe.matmul(dst, H3H[:, n - HB, :], adj_high, start=True, stop=False)
                    pe.matmul(dst, H3H[:, n - HB, :], adj_low, start=False, stop=False)
                    pe.matmul(dst, H3L[:, n - HB, :], adj_high, start=False, stop=True).then_inc(uk_mm, 1)

            def last_out(g, n, ps, plan):
                c, first, last = chunk_of(plan, n)
                pe.wait_ge(uk_sb, G * g + n + 1)
                for k in range(ADJ_PARTS):
                    mm = pe.matmul(as_batches(ps)[:, n - plan.chunks[c][0], :], UK[:, n % 4, k * T:(k + 1) * T],
                                   WL1[:, k, :], start=(k == 0), stop=(k == ADJ_PARTS - 1))
                if last:
                    mm.then_inc(out_mm, 1)

            def last_piece(what, n, g, k, plan):
                c, first, last = chunk_of(plan, n)
                if what == ADJP:
                    if n in plan.after_f:
                        pe.wait_ge(gate_act, GATES * g + GATES + GATES_BEFORE[last_unit(k, 0)] + F_READ)
                    elif n:
                        pe.wait_ge(uk_sb, G * g + n)
                    last_uk(g, n, bank(0, F))
                else:
                    if n in plan.after_f:
                        pe.wait_ge(gate_act, GATES * g + GATES + GATES_BEFORE[last_unit(k, 1)] + F_READ)
                    elif first and n:
                        pe.wait_ge(out_ready, CHUNKS * g + c)
                    last_out(g, n, bank(1, F), plan)

            pe.wait_ge(w_adj, 16)
            graph_u(0, 0)
            pe.wait_ge(consts, 2)
            pe.matmul(bank(0, 0)[:, 0:T], ONES[:, :], ADJ[:, :], start=True, stop=True).then_inc(rowsum_mm, 1)
            graph_u(1, 0)
            pe.wait_ge(bias_ready, 2)
            pe.wait_ge(w_gcn, 6 * 16)
            for s in range(STREAMS):
                graph_z(s, 0, False)
            for s in range(STREAMS):
                graph_y(s, 0)
            for s in range(STREAMS):
                graph_v(s, 0)

            def units(i, plan):
                for k in range(len(UNITS)):
                    unit(k, i, plan)

            def next_graph(i):
                pe.wait_ge(gate_act, GATES * i + GATES_BEFORE[LAST_OF[0]] + len(LATER_STEP))
                graph_u(0, i + 1)
                transpose_h(0, i)
                pe.wait_ge(gate_act, GATES * i + GATES)
                graph_u(1, i + 1)
                transpose_h(1, i)
                graph_z(0, i + 1, True)
                graph_z(1, i + 1, True)
                for s in range(STREAMS):
                    graph_y(s, i + 1)
                for s in range(STREAMS):
                    graph_v(s, i + 1)

            units(0, None)
            pe.wait_ge(consts, 10)
            pe.wait_ge(w_late, 32)
            next_graph(0)
            with pe.Fori(1, GROUPS - 1) as i:
                units(i, STEADY)
                next_graph(i)
            i = GROUPS - 1
            units(i, LATE)
            ring = [bank(0, 2), bank(0, 3), bank(1, 2), bank(1, 3)]
            pe.wait_ge(gate_act, GATES * i + GATES_BEFORE[LAST_OF[0]] + len(LATER_STEP))
            last_uk(i - 1, TAIL[0], ring[0])
            transpose_h(0, i)
            last_uk(i - 1, TAIL[1], ring[1])
            pe.wait_ge(gate_act, GATES * i + GATES)
            last_uk(i - 1, TAIL[2], ring[2])
            last_out(i - 1, TAIL[0], ring[3], LATE)
            transpose_h(1, i)
            last_uk(i - 1, TAIL[3], ring[0])
            for n in TAIL[1:]:
                last_out(i - 1, n, ring[3], LATE)

            out_ring = [bank(0, 0), bank(0, 1), bank(1, 0), bank(1, 1)]
            lag = 2
            for n in range(G + lag):
                if n == 3:
                    pe.wait_ge(out_ready, CHUNKS * i)
                if n < G:
                    last_uk(i, n, ring[n % 4])
                if n >= lag:
                    c, first, last = chunk_of(STEADY, n - lag)
                    if first and c >= 4:
                        pe.wait_ge(out_ready, CHUNKS * i + c - 3)
                    last_out(i, n - lag, out_ring[c % 4], STEADY)

        @block.scalar
        def _(act):
            def relu_h0(s, g):
                act.wait_ge(norm1, G * (g - 1) + HB * (s + 1))
                part = H0[:, s * HB:(s + 1) * HB, :]
                act.activation(part, part, ACT.Relu).then_inc(h0_ready, 1)

            def copy_u(s, g):
                for n in range(HBANKS):
                    act.wait_ge(u_mm, 2 * HBANKS * g + s * HBANKS + n + 1)
                    act.activation(U[:, s, 512 * n:512 * n + 512], bank(s, 2 + n), ACT.Copy).then_inc(u_sb, 1)

            def relu_z(s, g):
                for n in range(HBANKS):
                    act.wait_ge(z_sb, 2 * HBANKS * g + s * HBANKS + n + 1)
                    part = Z[:, s, 512 * n:512 * n + 512]
                    act.activation(part, part, ACT.Relu).then_inc(h1_ready, 1)

            def high_h(s, g):
                for n in range(HBANKS):
                    act.wait_ge(v_mm, 2 * HBANKS * g + s * HBANKS + n + 1)
                    act.activation(HH[:, s, :, n * PACK:(n + 1) * PACK].rearrange("p t b -> p b t"),
                                   as_batches(bank(s, n)), ACT.Relu).then_inc(h_high, 1)

            def norm_relu_h3(i, batches):
                act.wait_ge(shift2, i + 1)
                for b in batches:
                    act.activation(H3[:, b, :], X[:, i * G + b, :], ACT.Relu,
                                   bias=SHIFT2[:, b:b + 1], scale=RS2[:, b:b + 1]).then_inc(h3_first, 1)

            def copy_uk(g, n, ps):
                act.wait_ge(uk_mm, G * g + n + 1)
                act.activation(UK[:, n % 4, :], ps[:, 0:ADJ_PARTS * T], ACT.Copy).then_inc(uk_sb, 1)

            act.wait_ge(consts, 2)
            act.activation(TC[:, 0, 0:G], NHALF[:, :], ACT.Sigmoid)
            for b in range(G):
                if b % (G // QUARTERS) == 0:
                    act.wait_ge(shift1, b // (G // QUARTERS) + 1)
                act.activation(H0[:, b, :], X[:, b, :], ACT.Relu, bias=SHIFT1[:, b:b + 1],
                               scale=RS1[:, b:b + 1]).then_inc(h0_first, 1)
            copy_u(0, 0)
            copy_u(1, 0)
            for part in (relu_z, high_h):
                part(0, 0)
                part(1, 0)
            act.wait_ge(bias_ready, 1)

            def unit(k, i, plan):
                p, s, j, w0, nw, gates = UNITS[k]
                prev = last_unit(k, s)
                n = nw * HB
                if p == 1 and prev is not None:
                    act.wait_ge(lstm_step, STEPS * i + STEPS_BEFORE[prev] + STEPS_OF[prev] - 1)
                for m, q in enumerate(gates):
                    for what, b in plan.at.get((k, m), ()) if plan else ():
                        if what == ADJP:
                            copy_uk(i - 1, b, bank(0, F))
                    act.wait_ge(gate_mm, GATES * i + GATES_BEFORE[k] + m + 1)
                    act.activation(GT[:, s, q, 0:n], bank(s, q)[:, 0:n],
                                   ACT.Tanh if q == C else ACT.Sigmoid,
                                   bias=BG[:, 4 * (p - 1) + q:4 * (p - 1) + q + 1]).then_inc(gate_act, 1)
                for what, b in plan.at.get((k, len(gates)), ()) if plan else ():
                    if what == ADJP:
                        copy_uk(i - 1, b, bank(0, F))
                if plan is LATE and k == len(UNITS) - 1:
                    copy_uk(i - 1, TAIL[0], bank(0, 2))
                act.wait_ge(cell_ready, len(UNITS) * i + k + 1)
                act.activation(TC[:, s, 0:n], CS[:, s, 0:n], ACT.Tanh).then_inc(tanh_ready, 1)

            def units(i, more, plan):
                for k in range(len(UNITS)):
                    unit(k, i, plan)
                    if more and k in LN_RELU_AT:
                        relu_h0(LN_RELU_AT[k], i + 1)

            def next_graph(i):
                for part in (copy_u, relu_z):
                    part(0, i + 1)
                    part(1, i + 1)
                norm_relu_h3(i, range(HB))
                high_h(0, i + 1)
                high_h(1, i + 1)

            units(0, True, None)
            next_graph(0)
            with act.Fori(1, GROUPS - 1) as i:
                units(i, True, STEADY)
                next_graph(i)
            i = GROUPS - 1
            units(i, False, LATE)
            ring = [bank(0, 2), bank(0, 3), bank(1, 2), bank(1, 3)]
            for n in TAIL[1:]:
                copy_uk(i - 1, n, ring[(n - TAIL[0]) % 3])
            ahead = 3
            norm_relu_h3(i, range(ahead))
            for n in range(G):
                if n + ahead < HB:
                    norm_relu_h3(i, [n + ahead])
                copy_uk(i, n, ring[n % 4])

        @block.vector
        def _(dve):
            def stats1(g, batches):
                for b in batches:
                    dve.bn_stats(ST1[:, b, :], X[:, g * G + b, :]).then_inc(bn1, 1)

            def combine(st, done, count, before, minus, ve, var, lo, hi):
                diff, total, spread, square, both = (LN[:, n, lo:hi] for n in range(5))
                dve.wait_ge(done, count)
                dve.tensor_tensor(diff, st[:, lo:hi, 1], st[:, lo:hi, 4], ALU.subtract).then_inc(ln_step, 1)
                dve.tensor_tensor(total, st[:, lo:hi, 1], st[:, lo:hi, 4], ALU.add).then_inc(ln_step, 1)
                dve.tensor_tensor(spread, st[:, lo:hi, 2], st[:, lo:hi, 5], ALU.add).then_inc(ln_step, 1)
                dve.wait_ge(ln_step, before + 1)
                dve.tensor_tensor(square, diff, diff, ALU.mult).then_inc(ln_step, 1)
                dve.wait_ge(ln_step, before + 2)
                dve.tensor_scalar(minus[:, lo:hi], total, -0.5, None, ALU.mult).then_inc(var, 1)
                dve.wait_ge(ln_step, before + 4)
                dve.scalar_tensor_tensor(out=both, in0=square, scalar=D / 4, in1=spread,
                                         op0=ALU.mult, op1=ALU.add).then_inc(ln_step, 1)
                dve.wait_ge(ln_step, before + 5)
                dve.tensor_scalar(ve[:, lo:hi], both, 1 / D, EPS, ALU.mult, ALU.add).then_inc(var, 1)

            def norm_h0(g, ready, batches):
                dve.wait_ge(rs1, ready)
                for b in batches:
                    dve.tensor_scalar(H0[:, b, :], X[:, g * G + b, :], MINUS1[:, b:b + 1], RS1[:, b:b + 1],
                                      ALU.add, ALU.mult).then_inc(norm1, 1)

            def bias_z(s, g):
                for n in range(HBANKS):
                    dve.wait_ge(z_mm, 2 * HBANKS * g + s * HBANKS + n + 1)
                    dve.tensor_tensor(as_batches(Z[:, s, 512 * n:512 * n + 512]), as_batches(bank(s, n)),
                                      BG0T[:, :].unsqueeze(1).broadcast_to([128, PACK, T]),
                                      ALU.add).then_inc(z_sb, 1)

            def bias_y(s, g):
                for n in range(HBANKS):
                    dve.wait_ge(y_mm, 2 * HBANKS * g + s * HBANKS + n + 1)
                    dve.tensor_tensor(as_batches(Y[:, s, 512 * n:512 * n + 512]), as_batches(bank(s, 2 + n)),
                                      BG1[:, :].unsqueeze(1).broadcast_to([128, PACK, D]),
                                      ALU.add).then_inc(y_sb, 1)

            def low_h(s, g):
                for n in range(HBANKS):
                    dve.wait_ge(h_high, 2 * HBANKS * g + s * HBANKS + n + 1)
                    part = slice(n * PACK, (n + 1) * PACK)
                    dve.scalar_tensor_tensor(out=HL[:, s, :, part].rearrange("p t b -> p b t"),
                                             in0=as_batches(bank(s, n)), scalar=0.0,
                                             in1=HH[:, s, :, part].rearrange("p t b -> p b t").bitcast(F32),
                                             op0=ALU.max, op1=ALU.subtract).then_inc(h_low, 1)

            def unit_cell(k, i):
                p, s, j, w0, nw, gates = UNITS[k]
                n = nw * HB
                done = GATES * i + GATES_BEFORE[k]
                steps = STEPS * i + STEPS_BEFORE[k]
                dve.wait_ge(gate_act, done + 2)
                if j == 0:
                    dve.tensor_tensor(CS[:, s, 0:n], GT[:, s, I, 0:n], GT[:, s, C, 0:n],
                                      ALU.mult).then_inc(cell_ready, 1)
                    return
                dve.tensor_tensor(IC[:, s, 0:n], GT[:, s, I, 0:n], GT[:, s, C, 0:n],
                                  ALU.mult).then_inc(lstm_step, 1)
                dve.wait_ge(gate_act, done + 3)
                dve.tensor_tensor(CS[:, s, 0:n], GT[:, s, F, 0:n], CS[:, s, 0:n],
                                  ALU.mult).then_inc(lstm_step, 1)
                dve.wait_ge(lstm_step, steps + 2)
                dve.tensor_tensor(CS[:, s, 0:n], IC[:, s, 0:n], CS[:, s, 0:n],
                                  ALU.add).then_inc(cell_ready, 1)

            def hidden_parts(k):
                p, s, j, w0, nw, gates = UNITS[k]
                n = nw * HB
                if j == p - 1:
                    return (windows(HH, s, p, j, w0, nw), windows(HL, s, p, j, w0, nw),
                            HT[:, s, 0:n].rearrange("p (w b) -> p w b", b=HB))
                return SH[:, s, 0:n], SL[:, s, 0:n], HT[:, s, 0:n]

            def unit_hidden(k, i):
                p, s, j, w0, nw, gates = UNITS[k]
                n = nw * HB
                steps = STEPS * i + STEPS_BEFORE[k] + STEPS_OF[k]
                high, low, full = hidden_parts(k)
                dve.wait_ge(tanh_ready, len(UNITS) * i + k + 1)
                dve.tensor_tensor(HT[:, s, 0:n], GT[:, s, O, 0:n], TC[:, s, 0:n],
                                  ALU.mult).then_inc(lstm_step, 1)
                dve.wait_ge(lstm_step, steps - 1)
                dve.tensor_copy(high, full).then_inc(lstm_step, 1)

            def unit_low(k, i):
                high, low, full = hidden_parts(k)
                dve.wait_ge(lstm_step, STEPS * i + STEPS_BEFORE[k] + STEPS_OF[k])
                dve.tensor_tensor(low, full, high.bitcast(F32), ALU.subtract).then_inc(h_out, 1)

            def add_x(s, i):
                for n in range(HBANKS):
                    dve.wait_ge(t_mm, 2 * HBANKS * i + s * HBANKS + n + 1)
                    part = bass.ds(i * G + s * HB + n * PACK, PACK)
                    dve.tensor_tensor(X[:, part, :], as_batches(bank(s, n)), X[:, part, :],
                                      ALU.add).then_inc(x2_ready, 1)

            def stats2(s, i):
                wait_apart(dve, x2_ready, 2 * HBANKS * i + HBANKS * (s + 1), x_quarter[0], 16)
                for b in range(s * HB, s * HB + HB):
                    dve.bn_stats(ST2[:, b, :], X[:, i * G + b, :]).then_inc(bn2, 1)

            def combine2(s, i, more):
                combine(ST2, bn2, G * i + HB * (s + 1), COMBINE * (QUARTERS + 3 * i + s + (1 if more else 0)),
                        MINUS2, VE2, var2, s * HB, s * HB + HB)

            def norm_h3(i):
                dve.wait_ge(rs2, STREAMS * i + 2)
                for b in range(HB, G):
                    dve.tensor_scalar(H3[:, b, :], X[:, i * G + b, :], MINUS2[:, b:b + 1], RS2[:, b:b + 1],
                                      ALU.add, ALU.mult).then_inc(norm2, 1)

            def split_h3(i):
                wait_apart(dve, norm2, HB * i + HB, x_quarter[0], 16)
                dve.tensor_scalar(H3H[:, :, :], H3[:, HB:G, :], 0.0, None, ALU.max).then_inc(h3_high, 1)
                wait_apart(dve, h3_high, i + 1, x_quarter[0], 16)
                dve.scalar_tensor_tensor(out=H3L[:, :, :], in0=H3[:, HB:G, :], scalar=0.0,
                                         in1=H3H[:, :, :].bitcast(F32),
                                         op0=ALU.max, op1=ALU.subtract).then_inc(h3_second, 1)

            def add_out(g, c, ps, plan):
                first, size = plan.chunks[c]
                dve.wait_ge(out_mm, CHUNKS * g + c + 1)
                dve.wait_ge(xb_ready, STREAMS * g + (first + size - 1) // HB + 1)
                part = bass.ds(g * G + first, size)
                dve.tensor_tensor(X[:, part, :], as_batches(ps)[:, 0:size, :], X[:, part, :],
                                  ALU.add).then_inc(out_ready, 1)

            for q in range(QUARTERS):
                lo, hi = q * G // QUARTERS, (q + 1) * G // QUARTERS
                dve.wait_ge(x_quarter[q], 16)
                stats1(0, range(lo, hi))
                combine(ST1, bn1, hi, COMBINE * q, MINUS1, VE1, var1, lo, hi)
            dve.wait_ge(w_gcn, 6 * 16)
            dve.tensor_tensor(BG[:, :], BI[:, :], BH[:, :], ALU.add).then_inc(bias_ready, 1)
            dve.wait_ge(rowsum_mm, 1)
            dve.tensor_scalar(BG0T[:, :], bank(0, 0)[:, 0:T], BG0[:, 0:1], None, ALU.mult).then_inc(bias_ready, 1)
            dve.wait_ge(bias_ready, 2)
            for part in (bias_z, bias_y, low_h):
                part(0, 0)
                part(1, 0)
            dve.wait_ge(x_rest, 16 * (GROUPS - 1))

            def units(i, more, plan):
                for k in range(len(UNITS)):
                    if plan and k in plan.read_ahead:
                        add_out(i - 1, plan.read_ahead[k], bank(1, F), plan)
                    if k not in CELL_EARLY:
                        unit_cell(k, i)
                    if plan and k in plan.read_after:
                        add_out(i - 1, plan.read_after[k], bank(1, F), plan)
                    if more and k in LN_STATS_AT:
                        stats1(i + 1, LN_STATS_AT[k])
                    if more and k == LN_COMBINE_AT:
                        combine(ST1, bn1, G * i + 2 * G, COMBINE * (QUARTERS + 3 * i),
                                MINUS1, VE1, var1, 0, G)
                    if more and k in LN_APPLY_AT:
                        norm_h0(i + 1, QUARTERS + i + 1, LN_APPLY_AT[k])
                    unit_hidden(k, i)
                    if k + 1 in CELL_EARLY:
                        unit_cell(k + 1, i)
                    unit_low(k, i)
                    if plan and k == NORM_AT:
                        norm_h3(i - 1)
                    if plan and k == SPLIT_AT:
                        split_h3(i - 1)

            def next_graph(i):
                add_x(0, i)
                stats2(0, i)
                add_x(1, i)
                bias_z(0, i + 1)
                combine2(0, i, True)
                bias_z(1, i + 1)
                bias_y(0, i + 1)
                bias_y(1, i + 1)
                stats2(1, i)
                low_h(0, i + 1)
                combine2(1, i, True)
                low_h(1, i + 1)

            units(0, True, None)
            next_graph(0)
            with dve.Fori(1, GROUPS - 1) as i:
                units(i, True, STEADY)
                next_graph(i)
            i = GROUPS - 1
            units(i, False, LATE)
            add_x(0, i)
            stats2(0, i)
            combine2(0, i, False)
            add_x(1, i)
            stats2(1, i)
            combine2(1, i, False)
            add_out(i - 1, CHUNKS - 1, bank(1, 3), LATE)
            norm_h3(i)
            split_h3(i)
            out_ring = [bank(0, 0), bank(0, 1), bank(1, 0), bank(1, 1)]
            for c in range(CHUNKS):
                add_out(i, c, out_ring[c % 4], STEADY)


def kernel(**inputs):
    import numpy as np
    import concourse.bacc as bacc
    from concourse import mybir as _mybir
    from concourse.bass_utils import run_bass_kernel_spmd

    a = {k: np.asarray(v) for k, v in inputs.items()}

    def gates_t(w):
        return w.transpose(2, 0, 1)

    laid_out = {
        "x_tbd": a["x"].transpose(1, 0, 2),
        "adj_t": a["adj"].T,
        "wg0": a["L0_gnn_Wg0"],
        "bg0_col": a["L0_gnn_bg0"].reshape(D, 1),
        "wg1": a["L0_gnn_Wg1"],
        "bg1": a["L0_gnn_bg1"],
        "wih_t": gates_t(a["L0_gnn_Wih"]),
        "whh_t": gates_t(a["L0_gnn_Whh"][1:]),
        "bih_t": a["L0_gnn_bih"].reshape(16, D).T,
        "bhh_t": a["L0_gnn_bhh"].reshape(16, D).T,
        "w_l1": a["L1_gnn_W"].transpose(1, 0, 2),
        "bias": a["L1_gnn_bias"],
    }
    nc = bacc.Bacc("TRN2", target_bir_lowering=False, num_devices=1)
    arrays, args = {}, []
    for name, v in laid_out.items():
        v = np.ascontiguousarray(v)
        arrays[name] = v
        args.append(nc.dram_tensor(name, v.shape, _mybir.dt.from_np(v.dtype), kind="ExternalInput").ap())
    args.append(nc.dram_tensor("out_tbd", (T, B, D), _mybir.dt.float32, kind="ExternalOutput").ap())
    program(nc, *args)
    r = run_bass_kernel_spmd(nc, [arrays], core_ids=[0])
    return np.ascontiguousarray(r.results[0]["out_tbd"].transpose(1, 0, 2))
```
